# Optimizing a Trainium2 kernel written in Bass

```python
import numpy as np
import jax
import jax.numpy as jnp

def _softmax(x, axis=-1):
    return jax.nn.softmax(x, axis=axis)

def _gelu(x):
    return jax.nn.gelu(x, approximate=True)

def _silu(x):
    return jax.nn.silu(x)

def _sigmoid(x):
    return jax.nn.sigmoid(x)

def _layernorm(x, axis=-1, eps=1e-05):
    m = jnp.mean(x, axis=axis, keepdims=True)
    v = jnp.var(x, axis=axis, keepdims=True)
    return (x - m) / jnp.sqrt(v + eps)

def _scatter_add(tgt, idx, src, axis=0):
    return tgt.at[idx].add(src)

def _segment_sum(src, seg, n):
    return jax.ops.segment_sum(src, seg, n)
kernel_name = 'mk_adj_resnorm_d4_adj_r2_a56669'

def setup_inputs(seed: int=0):
    np.random.seed(seed)
    _w = jnp.asarray

    def _rec_inputs():
        import jax
        import jax.numpy as jnp
        _gk = jax.random.key(seed)
        x = -0.0005207 + 1.001 * jax.random.normal(jax.random.fold_in(_gk, 1), (16, 512, 128), jnp.float32)
        _a = jax.random.bernoulli(jax.random.fold_in(_gk, 2), 0.015625, (16, 512, 512))
        _a = jnp.logical_or(_a, jnp.swapaxes(_a, -1, -2))
        _a = jnp.logical_or(_a, jnp.eye(512, dtype=bool))
        adj = _a.astype(jnp.int32)
        return (x, adj)
    x, adj = _rec_inputs()

    def _L0_gnn_setup():
        import jax, jax.numpy as jnp
        import numpy as np
        DIM = 128
        HEADS = 8
        HEAD_DIM = DIM // HEADS
        DFF = 4 * DIM
        EPS = 1e-05

        def _layernorm(x, g, b):
            m = jnp.mean(x, axis=-1, keepdims=True)
            v = jnp.mean(jnp.square(x - m), axis=-1, keepdims=True)
            return (x - m) * jax.lax.rsqrt(v + EPS) * g + b
        key = jax.random.key(seed)
        ks = jax.random.split(key, 12)
        B, N = (8, 512)
        s = 1.0 / np.sqrt(DIM)
        x = jax.random.normal(ks[0], (B, N, DIM), dtype=jnp.float32)
        adj = jax.random.randint(ks[1], (B, N, N), 0, 2, dtype=jnp.int32)
        return {'x': x, 'adj': adj, 'Wqkv': jax.random.normal(ks[2], (3 * DIM, DIM), jnp.float32) * s, 'bqkv': jnp.zeros((3 * DIM,), jnp.float32), 'Wo': jax.random.normal(ks[3], (DIM, DIM), jnp.float32) * s, 'bo': jnp.zeros((DIM,), jnp.float32), 'ln1_g': jnp.ones((DIM,), jnp.float32), 'ln1_b': jnp.zeros((DIM,), jnp.float32), 'W1': jax.random.normal(ks[4], (DFF, DIM), jnp.float32) * s, 'b1': jnp.zeros((DFF,), jnp.float32), 'W2': jax.random.normal(ks[5], (DIM, DFF), jnp.float32) * (1.0 / np.sqrt(DFF)), 'b2': jnp.zeros((DIM,), jnp.float32), 'ln2_g': jnp.ones((DIM,), jnp.float32), 'ln2_b': jnp.zeros((DIM,), jnp.float32)}
    _L0_gnn_all = _L0_gnn_setup()
    _L0_gnn_in = {k: v for k, v in _L0_gnn_all.items() if k in ('Wqkv', 'bqkv', 'Wo', 'bo', 'ln1_g', 'ln1_b', 'W1', 'b1', 'W2', 'b2', 'ln2_g', 'ln2_b')}
    del _L0_gnn_all

    def _L1_gnn_setup():
        import jax, jax.numpy as jnp
        import numpy as np
        B, N, D_IN, D_OUT, R = (8, 1024, 128, 128, 4)
        key = jax.random.key(seed)
        k1, k2, k3, k4 = jax.random.split(key, 4)
        x = jax.random.normal(k1, (B, N, D_IN), dtype=jnp.float32)
        adj = jnp.zeros((1,), dtype=jnp.float32)
        relation = jax.random.randint(k2, (B, N, N), 0, R + 1, dtype=jnp.int32)
        weight = jax.random.normal(k3, (R, D_IN, D_OUT), dtype=jnp.float32) * 0.05
        bias = jax.random.normal(k4, (D_OUT,), dtype=jnp.float32) * 0.05
        return {'x': x, 'adj': adj, 'relation': relation, 'weight': weight, 'bias': bias}
    _L1_gnn_all = _L1_gnn_setup()
    _L1_gnn_in = {k: v for k, v in _L1_gnn_all.items() if k in ('adj', 'weight', 'bias')}
    del _L1_gnn_all

    def _L2_gnn_setup():
        import jax, jax.numpy as jnp
        import numpy as np
        NEG_INF = -9000000000000000.0
        ALPHA = 0.2
        key = jax.random.key(seed)
        k1, k2, k3, k4 = jax.random.split(key, 4)
        B, N, Fin, Fout = (8, 1024, 128, 128)
        h = jax.random.normal(k1, (B, N, Fin), dtype=jnp.float32)
        adj = jax.random.randint(k2, (B, N, N), 0, 2, dtype=jnp.int32)
        W = jax.random.normal(k3, (Fin, Fout), dtype=jnp.float32) * 0.05
        a = jax.random.normal(k4, (2 * Fout, 1), dtype=jnp.float32) * 0.05
        return {'h': h, 'adj': adj, 'W': W, 'a': a}
    _L2_gnn_all = _L2_gnn_setup()
    _L2_gnn_in = {k: v for k, v in _L2_gnn_all.items() if k in ('W', 'a')}
    del _L2_gnn_all

    def _L3_gnn_setup():
        import jax, jax.numpy as jnp
        import numpy as np
        B, N, C_IN, H, C_OUT = (8, 512, 128, 4, 128)
        C = C_OUT // H
        ALPHA = 0.2
        NEG_INF = -9000000000000000.0
        key = jax.random.key(seed)
        k1, k2, k3, k4, k5 = jax.random.split(key, 5)
        node_feats = jax.random.normal(k1, (B, N, C_IN), dtype=jnp.float32)
        adj_matrix = jax.random.randint(k2, (B, N, N), 0, 2, dtype=jnp.int32)
        eye = jnp.eye(N, dtype=jnp.int32)[None]
        adj_matrix = jnp.maximum(adj_matrix, eye)

        def xavier(k, shape, fan_in, fan_out, gain=1.414):
            lim = gain * np.sqrt(6.0 / (fan_in + fan_out))
            return jax.random.uniform(k, shape, jnp.float32, -lim, lim)
        W = xavier(k3, (C_OUT, C_IN), C_IN, C_OUT)
        b = jnp.zeros((C_OUT,), dtype=jnp.float32)
        a = xavier(k4, (H, 2 * C), 2 * C, H)
        return {'node_feats': node_feats, 'adj_matrix': adj_matrix, 'W': W, 'b': b, 'a': a}
    _L3_gnn_all = _L3_gnn_setup()
    _L3_gnn_in = {k: v for k, v in _L3_gnn_all.items() if k in ('W', 'b', 'a')}
    del _L3_gnn_all
    return {'x': x, 'adj': adj, 'L0_gnn_Wqkv': _L0_gnn_in['Wqkv'], 'L0_gnn_bqkv': _L0_gnn_in['bqkv'], 'L0_gnn_Wo': _L0_gnn_in['Wo'], 'L0_gnn_bo': _L0_gnn_in['bo'], 'L0_gnn_ln1_g': _L0_gnn_in['ln1_g'], 'L0_gnn_ln1_b': _L0_gnn_in['ln1_b'], 'L0_gnn_W1': _L0_gnn_in['W1'], 'L0_gnn_b1': _L0_gnn_in['b1'], 'L0_gnn_W2': _L0_gnn_in['W2'], 'L0_gnn_b2': _L0_gnn_in['b2'], 'L0_gnn_ln2_g': _L0_gnn_in['ln2_g'], 'L0_gnn_ln2_b': _L0_gnn_in['ln2_b'], 'L1_gnn_adj': _L1_gnn_in['adj'], 'L1_gnn_weight': _L1_gnn_in['weight'], 'L1_gnn_bias': _L1_gnn_in['bias'], 'L2_gnn_W': _L2_gnn_in['W'], 'L2_gnn_a': _L2_gnn_in['a'], 'L3_gnn_W': _L3_gnn_in['W'], 'L3_gnn_b': _L3_gnn_in['b'], 'L3_gnn_a': _L3_gnn_in['a']}

def reference(x, adj, L0_gnn_Wqkv, L0_gnn_bqkv, L0_gnn_Wo, L0_gnn_bo, L0_gnn_ln1_g, L0_gnn_ln1_b, L0_gnn_W1, L0_gnn_b1, L0_gnn_W2, L0_gnn_b2, L0_gnn_ln2_g, L0_gnn_ln2_b, L1_gnn_adj, L1_gnn_weight, L1_gnn_bias, L2_gnn_W, L2_gnn_a, L3_gnn_W, L3_gnn_b, L3_gnn_a):
    import jax
    import jax.numpy as jnp

    def _L0_gnn_ref(x, adj, Wqkv, bqkv, Wo, bo, ln1_g, ln1_b, W1, b1, W2, b2, ln2_g, ln2_b):
        import jax, jax.numpy as jnp
        import numpy as np
        DIM = 128
        HEADS = 8
        HEAD_DIM = DIM // HEADS
        DFF = 4 * DIM
        EPS = 1e-05

        def _layernorm(x, g, b):
            m = jnp.mean(x, axis=-1, keepdims=True)
            v = jnp.mean(jnp.square(x - m), axis=-1, keepdims=True)
            return (x - m) * jax.lax.rsqrt(v + EPS) * g + b
        B, N, _ = x.shape
        eye = jnp.eye(N, dtype=bool)[None]
        allowed = (adj > 0) | (jnp.swapaxes(adj, 1, 2) > 0) | eye
        qkv = x @ Wqkv.T + bqkv
        q, k, v = jnp.split(qkv, 3, axis=-1)

        def heads(t):
            return t.reshape(B, N, HEADS, HEAD_DIM).transpose(0, 2, 1, 3)
        q, k, v = (heads(q), heads(k), heads(v))
        scale = 1.0 / np.sqrt(HEAD_DIM)
        scores = jnp.einsum('bhqd,bhkd->bhqk', q * scale, k)
        scores = jnp.where(allowed[:, None], scores, -jnp.inf)
        attn = jax.nn.softmax(scores, axis=-1)
        ctx = jnp.einsum('bhqk,bhkd->bhqd', attn, v)
        ctx = ctx.transpose(0, 2, 1, 3).reshape(B, N, DIM)
        attn_out = ctx @ Wo.T + bo
        x = _layernorm(x + attn_out, ln1_g, ln1_b)
        ff = jax.nn.relu(x @ W1.T + b1) @ W2.T + b2
        x = _layernorm(x + ff, ln2_g, ln2_b)
        return x

    def _L1_gnn_ref(x, adj, relation, weight, bias):
        import jax, jax.numpy as jnp
        import numpy as np
        B, N, D_IN, D_OUT, R = (8, 1024, 128, 128, 4)
        rel_ids = jnp.arange(1, weight.shape[0] + 1, dtype=relation.dtype)
        masks = (relation[None] == rel_ids[:, None, None, None]).astype(x.dtype)
        h = jnp.einsum('rbnm,bmd->rbnd', masks, x)
        y = jnp.einsum('rbnd,rdo->bno', h, weight)
        return y + bias

    def _L2_gnn_ref(h, adj, W, a):
        import jax, jax.numpy as jnp
        import numpy as np
        NEG_INF = -9000000000000000.0
        ALPHA = 0.2
        Fout = W.shape[1]
        Wh = jnp.matmul(h, W)
        a1 = a[:Fout, 0]
        a2 = a[Fout:, 0]
        s1 = jnp.einsum('bnf,f->bn', Wh, a1)
        s2 = jnp.einsum('bnf,f->bn', Wh, a2)
        e = jax.nn.leaky_relu(s1[:, :, None] + s2[:, None, :], negative_slope=ALPHA)
        attn = jnp.where(adj > 0, e, NEG_INF)
        attn = jax.nn.softmax(attn, axis=2)
        h_prime = jnp.matmul(attn, Wh)
        return h_prime

    def _L3_gnn_ref(node_feats, adj_matrix, W, b, a):
        import jax, jax.numpy as jnp
        import numpy as np
        B, N, C_IN, H, C_OUT = (8, 512, 128, 4, 128)
        C = C_OUT // H
        ALPHA = 0.2
        NEG_INF = -9000000000000000.0
        Bb, Nn, _ = node_feats.shape
        Hh, twoC = a.shape
        Cc = twoC // 2
        h = (node_feats @ W.T + b).reshape(Bb, Nn, Hh, Cc)
        a_src, a_dst = (a[:, :Cc], a[:, Cc:])
        l_src = jnp.einsum('bihc,hc->bih', h, a_src)
        l_dst = jnp.einsum('bjhc,hc->bjh', h, a_dst)
        logits = jax.nn.leaky_relu(l_src[:, :, None, :] + l_dst[:, None, :, :], ALPHA)
        logits = jnp.where(adj_matrix[..., None] == 1, logits, NEG_INF)
        probs = jax.nn.softmax(logits, axis=2)
        out = jnp.einsum('bijh,bjhc->bihc', probs, h)
        return out.reshape(Bb, Nn, Hh * Cc)
    x = _layernorm(x + _L0_gnn_ref(x, adj, L0_gnn_Wqkv, L0_gnn_bqkv, L0_gnn_Wo, L0_gnn_bo, L0_gnn_ln1_g, L0_gnn_ln1_b, L0_gnn_W1, L0_gnn_b1, L0_gnn_W2, L0_gnn_b2, L0_gnn_ln2_g, L0_gnn_ln2_b), axis=-1)
    x = _layernorm(x + _L1_gnn_ref(x, L1_gnn_adj, adj, L1_gnn_weight, L1_gnn_bias), axis=-1)
    x = _layernorm(x + _L2_gnn_ref(x, adj, L2_gnn_W, L2_gnn_a), axis=-1)
    x = _layernorm(x + _L3_gnn_ref(x, adj, L3_gnn_W, L3_gnn_b, L3_gnn_a), axis=-1)
    return x

_drawn_inputs = setup_inputs


def setup_inputs(seed=0):
    import zlib

    import numpy as np

    out = dict(_drawn_inputs(seed))
    spreads = {'L0_gnn_bqkv': (0.0, 0.1),
     'L0_gnn_bo': (0.0, 0.1),
     'L0_gnn_ln1_g': (1.0, 0.2),
     'L0_gnn_ln1_b': (0.0, 0.1),
     'L0_gnn_b1': (0.0, 0.1),
     'L0_gnn_b2': (0.0, 0.1),
     'L0_gnn_ln2_g': (1.0, 0.2),
     'L0_gnn_ln2_b': (0.0, 0.1),
     'L3_gnn_b': (0.0, 0.1)}
    factors = {'L1_gnn_bias': 3.024, 'L2_gnn_a': 3.127}
    for name, (base, spread) in spreads.items():
        noise = np.random.default_rng([zlib.crc32(name.encode()), seed]).standard_normal(out[name].shape)
        drawn = base * np.exp(spread * noise) if base else spread * noise
        out[name] = jnp.asarray(drawn.astype(out[name].dtype))
    for name, factor in factors.items():
        out[name] = (out[name] * factor).astype(out[name].dtype)
    return out
```

```python
import numpy as np
import concourse.bass as bass
from concourse import mybir
from contextlib import ExitStack

B, N, D = 16, 512, 128
P = 128
C = N // P
H0, DH = 8, 16
G0 = 2
DFF = 512
F = DFF // P
R = 4
H3, DC = 4, 32
EPS = 1e-5
ALPHA = 0.2
NEG_INF = -9000000000000000.0
NEG_L0 = -1.0e30
BIG = 3.0e38
START = 1

WORK = (["q0", "q1", "k0", "k1", "v", "ctx0", "ctx1", "ctxT", "wo", "x1T"] + [f"up{f}" for f in range(F)]
        + ["down", "y0T"] + [f"yw{c}" for c in range(C)] + ["rel", "relT", "y1T", "wh", "s2", "pv2", "y2T", "h3",
                                                           "s3", "pv3"])
TILES0 = [(0, h, c) for h in range(H0) for c in range(C)]
TILES2 = [(2, 0, c) for c in range(C)]
TILES3 = [(3, h, c) for h in range(H3) for c in range(C)]
TILES = TILES0 + TILES2 + TILES3
SCORES = TILES0 + [(2, 0)] + [(3, h) for h in range(H3)]
LN = 6


def build(nc, x, xT, adj, adjT, wqT, wkT, wvT, bq, bk, bv, woT, bo, w1T, b1, w2T, b2, ln1g, ln1b, ln2g, ln2b,
          rel_w, rel_b, w2g, w2gT, a2g, w3T, w3, b3c, b3r, a3, out):
    f32, bf16, i32 = mybir.dt.float32, mybir.dt.bfloat16, mybir.dt.int32
    ALU, ACT = mybir.AluOpType, mybir.ActivationFunctionType

    with ExitStack() as ctx:
        def sb(name, shape, dt=f32):
            return ctx.enter_context(nc.sbuf_tensor(name, shape, dt))

        def sem(name):
            return ctx.enter_context(nc.semaphore(name))

        def bank(name, shape=(P, 512)):
            return ctx.enter_context(nc.psum_tensor(name, list(shape), f32))

        wq_s, wk_s = sb("wq_s", [P, G0, P]), sb("wk_s", [P, G0, P])
        bq_s, bk_s = sb("bq_s", [P, G0]), sb("bk_s", [P, G0])
        wv_s, bv_s = sb("wv_s", [P, P]), sb("bv_s", [P, P])
        wo_s, bo_s = sb("wo_s", [P, P]), sb("bo_s", [P, P])
        w1_s, b1_s = sb("w1_s", [P, DFF]), sb("b1_s", [P, F])
        w2_s, b2_s = sb("w2_s", [P, F, P]), sb("b2_s", [P, P])
        ln1g_s, ln1b_s = sb("ln1g_s", [P, P]), sb("ln1b_s", [P, P])
        ln2g_s, ln2b_s = sb("ln2g_s", [P, P]), sb("ln2b_s", [P, P])
        relw_s, relb_s = sb("relw_s", [P, R * P]), sb("relb_s", [P, 1])
        w2g_s, w2gT_s, a2_s = sb("w2g_s", [P, P]), sb("w2gT_s", [P, P]), sb("a2_s", [P, 2])
        w3T_s, w3_s = sb("w3T_s", [P, P]), sb("w3_s", [P, P])
        b3c_s, b3r_s, a3_s = sb("b3c_s", [P, 1]), sb("b3r_s", [P, P]), sb("a3_s", [P, 2 * H3])
        LOADS = [(wq_s, wqT), (wk_s, wkT), (bq_s, bq), (bk_s, bk), (wv_s, wvT), (bv_s, bv), (wo_s, woT), (bo_s, bo),
                 (w1_s, w1T), (b1_s, b1), (w2_s, w2T), (b2_s, b2), (ln1g_s, ln1g), (ln1b_s, ln1b), (ln2g_s, ln2g),
                 (ln2b_s, ln2b), (relw_s, rel_w), (relb_s, rel_b), (w2g_s, w2g), (w2gT_s, w2gT), (a2_s, a2g),
                 (w3T_s, w3T), (w3_s, w3), (b3c_s, b3c), (b3r_s, b3r), (a3_s, a3)]
        ident = sb("ident", [P, P])
        offdiag = sb("offdiag", [P, C, 512], bf16)
        half_neg = sb("half_neg", [P, C])
        b3w = sb("b3w", [P, P])
        wa_s = sb("wa_s", [P, 2 + 2 * H3])
        wd_s = sb("wd_s", [P, 1 + H3, P])
        c3 = sb("c3", [P, 2 * H3])
        c3s = sb("c3s", [P, H3])

        xT_s, x_s = sb("xT_s", [P, 512]), sb("x_s", [P, C, P])
        adj_s, adjT_s = sb("adj_s", [P, C, 512], i32), sb("adjT_s", [P, C, 512], i32)
        bias0, bias2, bias3 = (sb(f"bias{k}", [P, C, 512], bf16) for k in (0, 2, 3))
        relT = sb("relT", [P, R, C, 512], bf16)
        qT, kT = sb("qT", [P, G0, 512]), sb("kT", [P, G0, 512])
        V = sb("V", [P, C * H0, 32])
        masked = sb("masked", [P, 2, 512])
        probs = sb("probs", [P, 2, 512])
        probsT_flat = sb("probsT", [P, 2 * 4 * C * 512])
        probsT = probsT_flat.rearrange("p (u h c i) -> p u h c i", u=2, h=4, c=C)
        leaky = sb("leaky", [P, 2, 512])
        targets = sb("targets", [P, 2, 512])
        low = sb("low", [P, 2, 512])
        negmax, den, rden = (sb(n, [P, len(TILES)]) for n in ("negmax", "den", "rden"))
        ctx_s = sb("ctx_s", [P, G0, 512])
        rden0 = sb("rden0", [P, G0, C, 4])
        ctxn, ctxnT = sb("ctxn", [P, C, H0, DH]), sb("ctxnT", [P, 512])
        waited = sb("waited", [P, 1])
        t_s, u_s = sb("t_s", [P, C, P]), sb("u_s", [P, C, P])
        stats, mv = sb("stats", [P, C, 6]), sb("mv", [P, C, 2])
        vare, rstd = sb("vare", [P, C]), sb("rstd", [P, C])
        x1, x1T, hT = sb("x1", [P, C, P]), sb("x1T", [P, 512]), sb("hT", [P, F, 512])
        y0T = y1T = y2T = x1T
        x2 = sb("x2", [P, C, P])
        y0 = sb("y0", [P, C, P])
        yrest = sb("yrest", [P, R * P])
        ysplit = probsT_flat[:, C * 512:C * 512 + C * 3 * R * P // 2].bitcast(bf16)\
            .rearrange("p (c s n) -> p c s n", c=C, s=3)
        adjmax = ysplit[:, :, 0, :]
        relo = pv3_s = ctxnT
        y1 = sb("y1", [P, C, P])
        wh = sb("wh", [P, C, P])
        s_c, s_low = sb("s_c", [P, C, 1 + H3]), sb("s_low", [P, C, 1 + H3])
        y2 = sb("y2", [P, C, P])
        h3 = wh
        y3 = sb("y3", [P, C, P])

        scores = [bank(f"scores_ps{k}") for k in range(2)]
        tr = [bank(f"tr_ps{k}") for k in range(2)]
        acc = bank("acc_ps")
        work = [bank(f"work_ps{k}") for k in range(3)]

        weights_loaded = sem("weights_loaded")
        pool_const, dve_const, prep_ps, prep_sb = (sem(n) for n in ("pool_const", "dve_const", "prep_ps", "prep_sb"))
        xT_loaded, x_loaded, adj_loaded = sem("xT_loaded"), sem("x_loaded"), sem("adj_loaded")
        masks_ready, x_used = sem("masks_ready"), sem("x_used")
        work_done = sem("work_done")
        work_out = [sem(f"work_out{k}") for k in range(3)]
        scores_done = sem("scores_done")
        d_copied = sem("d_copied")
        low_done = sem("low_done")
        masked_done = sem("masked_done")
        exp_done = sem("exp_done")
        turned = sem("turned")
        probsT_act, probsT_dve = sem("probsT_act"), sem("probsT_dve")
        acc_done, acc_out = sem("acc_done"), sem("acc_out")
        ctxn_ready = sem("ctxn_ready")
        ln_var, ln_rstd, ln_out = sem("ln_var"), sem("ln_rstd"), sem("ln_out")
        yhi, ymid, ylo = sem("yhi"), sem("ymid"), sem("ylo")
        stored, y3_free = sem("stored"), sem("y3_free")
        dve_chain = sem("dve_chain")

        STARTED = [masks_ready, x_used, *work_out, masked_done, exp_done, turned, probsT_act, probsT_dve, acc_out,
                   ylo, d_copied, y3_free]

        NT, NW = len(TILES), len(WORK)

        def uses(b, name):
            n = WORK.index(name)
            return work_out[n % 3], START + b * len(range(n % 3, NW, 3)) + n // 3

        def out_of(b, name):
            s, n = uses(b, name)
            return s, n + 1

        def before(b, total, n, slots=2):
            return START + b * total + max(n - slots + 1, 0)

        block = ctx.enter_context(nc.Block())

        def flat(t):
            return t.rearrange("p c d -> p (c d)")

        def chunks(t):
            return t.rearrange("p (c d) -> p c d", c=C)

        def each_chunk(row):
            return row[:].unsqueeze(1).broadcast_to([P, C, P])

        @block.sync
        def _(sp):
            for dst, src in LOADS:
                sp.dma_start(dst[:], src).then_inc(weights_loaded, 16)
            with sp.Fori(0, B) as b:
                sp.wait_ge(masks_ready, START + b)
                sp.dma_start(adj_s[:], adj[b].rearrange("(c p) j -> p c j", p=P)).then_inc(adj_loaded, 16)
                sp.dma_start(adjT_s[:], adjT[b].rearrange("(c p) j -> p c j", p=P)).then_inc(adj_loaded, 16)
                sp.wait_ge(x_used, START + b)
                sp.dma_start(xT_s[:], xT[b]).then_inc(xT_loaded, 16)
                sp.dma_start(x_s[:], x[b].rearrange("(c p) d -> p c d", p=P)).then_inc(x_loaded, 16)
            sp.wait_ge(stored, B * 16)

        @block.gpsimd
        def _(pool):
            for s in STARTED:
                nc.gpsimd.sem_inc(s, START)
            nc.gpsimd.memset(ident[:], 0.0).then_inc(pool_const, 1)
            nc.gpsimd.memset(offdiag[:], NEG_L0).then_inc(pool_const, 1)
            nc.gpsimd.memset(half_neg[:], -0.5).then_inc(pool_const, 1)
            pool.wait_ge(pool_const, 3)
            nc.gpsimd.affine_select(out=ident[:], in_=ident[:], compare_op=ALU.not_equal, fill=1.0, base=0,
                                    pattern=[[-1, P]], channel_multiplier=1).then_inc(pool_const, 1)
            nc.gpsimd.affine_select(out=offdiag[:], in_=offdiag[:], compare_op=ALU.not_equal, fill=0.0, base=0,
                                    pattern=[[P, C], [-1, 512]], channel_multiplier=1).then_inc(pool_const, 1)
            pool.wait_ge(pool_const, 5)
            with pool.Fori(0, B) as b:
                for n in range(LN):
                    pool.wait_ge(ln_var, b * LN + n + 1)
                    nc.gpsimd.tensor_tensor(rstd[:], vare[:], half_neg[:], ALU.pow).then_inc(ln_rstd, 1)
                pool.wait_ge(ln_out, b * LN + LN)
                pool.dma_start(out[b].rearrange("(c p) d -> p c d", p=P), y3[:]).then_inc(stored, 16)
                pool.wait_ge(stored, b * 16 + 16)
                nc.gpsimd.sem_inc(y3_free, 1)

        @block.tensor
        def _(pe):
            pe.wait_ge(weights_loaded, 16 * len(LOADS))
            pe.wait_ge(dve_const, 2)
            pe.wait_ge(pool_const, 5)
            nc.tensor.matmul(work[0][:, 0:2], w2gT_s[:], a2_s[:], start=True, stop=True)
            nc.tensor.matmul(work[0][:, 2:2 + 2 * H3], w3_s[:], a3_s[:], start=True, stop=True)
            nc.tensor.matmul(work[0][:, 16:16 + 2 * H3], b3w[:], a3_s[:], start=True, stop=True).then_inc(prep_ps, 1)
            pe.wait_ge(prep_sb, 1)

            with pe.Fori(0, B) as b:
                def begin(name):
                    pe.wait_ge(*uses(b, name))
                    return work[WORK.index(name) % 3]

                def transposes(name, src):
                    w = begin(name)
                    for c in range(C):
                        ins = nc.tensor.transpose(w[:, c * P:(c + 1) * P], src(c), ident[:])
                    ins.then_inc(work_done, 1)

                def project(name, xt, w_s):
                    w = begin(name)
                    for c in range(C):
                        ins = nc.tensor.matmul(w[:, c * P:(c + 1) * P], xt[:, c * P:(c + 1) * P], w_s,
                                               start=True, stop=True)
                    ins.then_inc(work_done, 1)

                def turn(t):
                    pe.wait_ge(exp_done, START + b * NT + t + 1)
                    pe.wait_ge((probsT_act, probsT_dve)[t % 2], START + b * (NT // 2) + t // 2)
                    for c in range(C):
                        ins = nc.tensor.transpose(tr[t % 2][:, c * P:(c + 1) * P],
                                                  probs[:, t % 2, c * P:(c + 1) * P], ident[:])
                    ins.then_inc(turned, 1)

                def probsT_full(tiles):
                    pe.wait_ge(probsT_act, START + b * (NT // 2) + tiles // 2)
                    pe.wait_ge(probsT_dve, START + b * (NT // 2) + tiles // 2)

                def pv(n, buf, tiles, value):
                    probsT_full(tiles)
                    pe.wait_ge(acc_out, START + b * 3 + n)
                    for c in range(C):
                        for h in range(4):
                            ins = nc.tensor.matmul(acc[32 * h:32 * h + 32, :], value(c, h), probsT[:, buf, h, c, :],
                                                   start=(c == 0), stop=(c == C - 1), tile_position=(0, 32 * h))
                    ins.then_inc(acc_done, 1)

                pe.wait_ge(xT_loaded, b * 16 + 16)
                for name, w_s, g in (("q0", wq_s, 0), ("q1", wq_s, 1), ("k0", wk_s, 0), ("k1", wk_s, 1)):
                    w = begin(name)
                    nc.tensor.matmul(w[:], w_s[:, g, :], xT_s[:], start=True, stop=True).then_inc(work_done, 1)
                project("v", xT_s, wv_s[:])
                for name in ("q0", "q1", "k0", "k1", "v"):
                    pe.wait_ge(*out_of(b, name))
                n0 = len(TILES0)
                for t in range(n0 + 1):
                    if t < n0:
                        _l, h, c = TILES0[t]
                        g, r = h // 4, 32 * (h % 4)
                        pe.wait_ge(masked_done, before(b, NT, t))
                        nc.tensor.matmul(scores[t % 2][:], qT[r:r + 32, g, c * P:(c + 1) * P], kT[r:r + 32, g, :],
                                         start=True, stop=True).then_inc(scores_done, 1)
                    if t >= 1:
                        turn(t - 1)
                    if t == n0 // 2 + 2:
                        pv(0, 0, n0 // 2, lambda c, h: V[:, c * H0 + h, :])
                pv(1, 1, n0, lambda c, h: V[:, c * H0 + 4 + h, :])
                for g in range(G0):
                    pe.wait_ge(acc_out, START + b * 3 + g + 1)
                    transposes(f"ctx{g}", lambda c: ctx_s[:, g, c * P:(c + 1) * P])
                pe.wait_ge(*out_of(b, "ctx0"))
                pe.wait_ge(*out_of(b, "ctx1"))
                transposes("ctxT", lambda c: ctxn[:, c, :, :].rearrange("p h d -> p (h d)"))
                pe.wait_ge(*out_of(b, "ctxT"))
                project("wo", ctxnT, wo_s[:])
                pe.wait_ge(ln_out, b * LN + 1)
                transposes("x1T", lambda c: x1[:, c, :])
                pe.wait_ge(*out_of(b, "x1T"))
                for f in range(F):
                    w = begin(f"up{f}")
                    nc.tensor.matmul(w[:], w1_s[:, f * P:(f + 1) * P], x1T[:], start=True, stop=True)\
                        .then_inc(work_done, 1)
                for f in range(F):
                    pe.wait_ge(*out_of(b, f"up{f}"))
                w = begin("down")
                for c in range(C):
                    for f in range(F):
                        ins = nc.tensor.matmul(w[:, c * P:(c + 1) * P], hT[:, f, c * P:(c + 1) * P], w2_s[:, f, :],
                                               start=(f == 0), stop=(f == F - 1))
                ins.then_inc(work_done, 1)
                pe.wait_ge(ln_out, b * LN + 3)
                transposes("y0T", lambda c: y0[:, c, :])
                pe.wait_ge(*out_of(b, "y0T"))
                for c in range(C):
                    w = begin(f"yw{c}")
                    nc.tensor.matmul(w[:], y0T[:, c * P:(c + 1) * P], relw_s[:], start=True, stop=True)\
                        .then_inc(work_done, 1)
                w = begin("rel")
                pe.wait_ge(masks_ready, START + b + 1)
                for c in range(C):
                    pe.wait_ge(ylo, START + b * C + c + 1)
                    for part in range(3):
                        for r in range(R):
                            ins = nc.tensor.matmul(w[:], ysplit[:, c, part, r * P:(r + 1) * P], relT[:, r, c, :],
                                                   start=(c == part == r == 0),
                                                   stop=(c == C - 1 and part == 2 and r == R - 1))
                ins.then_inc(work_done, 1)
                pe.wait_ge(*out_of(b, "rel"))
                transposes("relT", lambda c: relo[:, c * P:(c + 1) * P])

                def attend(first, tiles, xt, s_name, wh_name, w_s, s_cols):
                    project(wh_name, xt, w_s)
                    w = begin(s_name)
                    k = s_cols.stop - s_cols.start
                    for c in range(C):
                        ins = nc.tensor.matmul(w[:, c * k:c * k + k], xt[:, c * P:(c + 1) * P], wa_s[:, s_cols],
                                               start=True, stop=True)
                    ins.then_inc(work_done, 1)
                    for t in range(len(tiles) + 1):
                        if t < len(tiles) and t % C == 0:
                            layer, h, _c = tiles[t]
                            n = SCORES.index((layer, h))
                            pe.wait_ge(masked_done, START + b * NT + n0)
                            pe.wait_ge(d_copied, START + b * (1 + H3) + max(n - n0 - 1, 0))
                            nc.tensor.matmul(scores[n % 2][:], wd_s[:, n - n0, :], xt[:], start=True,
                                             stop=True).then_inc(scores_done, 1)
                        if t >= 1:
                            turn(first + t - 1)

                pe.wait_ge(ln_out, b * LN + 4)
                transposes("y1T", lambda c: y1[:, c, :])
                pe.wait_ge(*out_of(b, "y1T"))
                attend(n0, TILES2, y1T, "s2", "wh", w2g_s[:], slice(0, 1))
                pe.wait_ge(*out_of(b, "wh"))
                w = begin("pv2")
                probsT_full(n0 + C)
                for c in range(C):
                    for cj in range(C):
                        ins = nc.tensor.matmul(w[:, c * P:(c + 1) * P], probsT[:, 0, 0, cj, c * P:(c + 1) * P],
                                               wh[:, cj, :], start=(cj == 0), stop=(cj == C - 1))
                ins.then_inc(work_done, 1)
                pe.wait_ge(ln_out, b * LN + 5)
                transposes("y2T", lambda c: y2[:, c, :])
                pe.wait_ge(*out_of(b, "y2T"))
                attend(n0 + C, TILES3, y2T, "s3", "h3", w3T_s[:], slice(2, 2 + H3))
                pe.wait_ge(*out_of(b, "h3"))
                pv(2, 1, NT, lambda c, h: h3[:, c, h * DC:(h + 1) * DC])
                pe.wait_ge(acc_out, START + b * 3 + 3)
                transposes("pv3", lambda c: pv3_s[:, c * P:(c + 1) * P])

        @block.scalar
        def _(act):
            act.wait_ge(weights_loaded, 16 * len(LOADS))
            with act.Fori(0, B) as b:
                def take(name):
                    n = WORK.index(name)
                    act.wait_ge(work_done, b * NW + n + 1)
                    return work[n % 3], work_out[n % 3]

                def copy(name, dst):
                    w, read = take(name)
                    nc.scalar.activation(dst, w[:], ACT.Copy).then_inc(read, 1)

                def exps(t):
                    act.wait_ge(masked_done, START + b * NT + t + 1)
                    act.wait_ge(turned, before(b, NT, t))
                    nc.scalar.activation(probs[:, t % 2, :], masked[:, t % 2, :], ACT.Exp, bias=negmax[:, t:t + 1],
                                         scale=-1.0, accum_out=den[:, t:t + 1]).then_inc(exp_done, 1)

                def evacuate(t, buf):
                    act.wait_ge(turned, START + b * NT + t + 1)
                    _l, h, c = TILES[t]
                    nc.scalar.activation(probsT[:, buf, h % 4, :, c * P:(c + 1) * P],
                                         tr[t % 2].rearrange("p (c i) -> p c i", c=C), ACT.Copy)\
                        .then_inc(probsT_act, 1)

                def sums(n, dst):
                    act.wait_ge(acc_done, b * 3 + n + 1)
                    nc.scalar.activation(dst, acc[:], ACT.Copy).then_inc(acc_out, 1)

                for g in range(G0):
                    w, read = take(f"k{g}")
                    nc.scalar.activation(kT[:, g, :], w[:], ACT.Identity, bias=bk_s[:, g:g + 1]).then_inc(read, 1)
                n0 = len(TILES0)
                for t in range(n0 + 1):
                    if t < n0:
                        exps(t)
                    if t >= 1 and (t - 1) % 2 == 0:
                        evacuate(t - 1, (t - 1) // 16)
                    if t == n0 // 2 + 4:
                        sums(0, ctx_s[:, 0, :])
                sums(1, ctx_s[:, 1, :])
                copy("ctxT", ctxnT[:])
                copy("x1T", x1T[:])
                for f in range(F):
                    w, read = take(f"up{f}")
                    nc.scalar.activation(hT[:, f, :], w[:], ACT.Relu, bias=b1_s[:, f:f + 1]).then_inc(read, 1)
                copy("y0T", y0T[:])
                for c in range(C):
                    act.wait_ge(work_done, b * NW + WORK.index(f"yw{c}") + 1)
                    nc.scalar.activation(ysplit[:, c, 0, :], work[WORK.index(f"yw{c}") % 3][:], ACT.Copy)\
                        .then_inc(yhi, 1)
                    act.wait_ge(*out_of(b, f"yw{c}"))
                    nc.scalar.activation(ysplit[:, c, 1, :], yrest[:], ACT.Copy).then_inc(ymid, 1)
                w, read = take("rel")
                nc.scalar.activation(relo[:], w[:], ACT.Identity, bias=relb_s[:]).then_inc(read, 1)

                def attend(first, tiles, k0, buf):
                    def lows(t):
                        layer, h, c = tiles[t]
                        n = SCORES.index((layer, h)) - n0
                        if c == 0:
                            act.wait_ge(scores_done, b * len(SCORES) + n0 + n + 1)
                            act.wait_ge(masked_done, START + b * NT + n0 + C * max(n - 1, 0))
                            nc.scalar.activation(targets[:, n % 2, :], scores[n % 2][:], ACT.Copy).then_inc(d_copied, 1)
                            act.wait_ge(d_copied, START + b * (1 + H3) + n + 1)
                        act.wait_ge(masked_done, START + b * NT + first + max(t - 1, 0))
                        nc.scalar.activation(low[:, t % 2, :], targets[:, n % 2, :], ACT.Identity,
                                             bias=s_low[:, c, k0 + h:k0 + h + 1], scale=ALPHA).then_inc(low_done, 1)
                    lows(0)
                    for t in range(len(tiles) + 1):
                        if t + 1 < len(tiles):
                            lows(t + 1)
                        if t < len(tiles):
                            exps(first + t)
                        if t >= 1 and (t - 1) % 2 == 0:
                            evacuate(first + t - 1, buf)

                copy("y1T", y1T[:])
                copy("wh", wh[:])
                act.wait_ge(*out_of(b, "s2"))
                attend(n0, TILES2, 0, 0)
                copy("y2T", y2T[:])
                act.wait_ge(*out_of(b, "s3"))
                attend(n0 + C, TILES3, 1, 1)
                sums(2, pv3_s[:])

        @block.vector
        def _(dve):
            nc.vector.memset(V[:], 1.0).then_inc(dve_const, 1)
            dve.wait_ge(weights_loaded, 16 * len(LOADS))
            nc.vector.tensor_copy(b3w[:], b3c_s[:].broadcast_to([P, P])).then_inc(dve_const, 1)
            dve.wait_ge(prep_ps, 1)
            nc.vector.tensor_copy(wa_s[:], work[0][:, 0:2 + 2 * H3]).then_inc(dve_const, 1)
            nc.vector.tensor_copy(c3[:], work[0][:, 16:16 + 2 * H3]).then_inc(dve_const, 1)
            dve.wait_ge(dve_const, 4)
            nc.vector.tensor_copy(wd_s[:, 0, :], wa_s[:, 1:2].broadcast_to([P, P])).then_inc(dve_const, 1)
            for h in range(H3):
                k = 2 + H3 + h
                nc.vector.tensor_copy(wd_s[:, 1 + h, :], wa_s[:, k:k + 1].broadcast_to([P, P])).then_inc(dve_const, 1)
            nc.vector.tensor_tensor(c3s[:], c3[:, 0:H3], c3[:, H3:2 * H3], ALU.add).then_inc(prep_sb, 1)
            dve.wait_ge(prep_sb, 1)
            dve.wait_ge(pool_const, 5)

            with dve.Fori(0, B) as b:
                nc.vector.sem_clear(dve_chain)
                chain = [0]

                def link(ins):
                    chain[0] += 1
                    ins.then_inc(dve_chain, 1)

                def linked():
                    dve.wait_ge(dve_chain, chain[0])

                def take(name):
                    n = WORK.index(name)
                    dve.wait_ge(work_done, b * NW + n + 1)
                    return work[n % 3], work_out[n % 3]

                def layernorm(n, src, dst, gain=None, shift=None):
                    linked()
                    for c in range(C):
                        link(nc.vector.bn_stats(stats[:, c, :], src[:, c, :]))
                    linked()
                    for c in range(C):
                        link(nc.vector.bn_aggr(mv[:, c, :], stats[:, c, :]))
                    linked()
                    nc.vector.tensor_scalar(vare[:], mv[:, :, 1], EPS, None, ALU.add).then_inc(ln_var, 1)
                    dve.wait_ge(ln_rstd, b * LN + n + 1)
                    if gain is None:
                        for c in range(C):
                            ins = nc.vector.tensor_scalar(dst[:, c, :], src[:, c, :], mv[:, c, 0:1], rstd[:, c:c + 1],
                                                          ALU.subtract, ALU.mult)
                            if c < C - 1:
                                link(ins)
                        ins.then_inc(ln_out, 1)
                    else:
                        for c in range(C):
                            link(nc.vector.tensor_scalar(dst[:, c, :], src[:, c, :], mv[:, c, 0:1], rstd[:, c:c + 1],
                                                         ALU.subtract, ALU.mult))
                        linked()
                        link(nc.vector.tensor_tensor(dst[:], dst[:], each_chunk(gain), ALU.mult))
                        linked()
                        nc.vector.tensor_tensor(dst[:], dst[:], each_chunk(shift), ALU.add).then_inc(ln_out, 1)

                dve.wait_ge(adj_loaded, b * 32 + 32)
                link(nc.vector.tensor_tensor(adjmax, adj_s[:], adjT_s[:], ALU.max))
                link(nc.vector.tensor_scalar(bias2[:], adj_s[:], 0.0, NEG_INF, ALU.is_le, ALU.mult))
                link(nc.vector.tensor_scalar(bias3[:], adj_s[:], 1.0, NEG_INF, ALU.not_equal, ALU.mult))
                for r in range(R):
                    ins = nc.vector.tensor_scalar(relT[:, r, :, :], adjT_s[:], float(r + 1), None, ALU.is_equal)
                    if r < R - 1:
                        link(ins)
                ins.then_inc(masks_ready, 1)
                linked()
                link(nc.vector.scalar_tensor_tensor(bias0[:], adjmax, 0.0, offdiag[:], ALU.is_le, ALU.mult))
                for g in range(G0):
                    w, read = take(f"q{g}")
                    nc.vector.tensor_scalar(qT[:, g, :], w[:], bq_s[:, g:g + 1], float(DH) ** -0.5, ALU.add, ALU.mult)\
                        .then_inc(read, 1)
                w, read = take("v")
                nc.vector.tensor_tensor(V.rearrange("p (c h) k -> p c h k", c=C)[:, :, :, 0:DH],
                                        w.rearrange("p (c h d) -> p c h d", c=C, h=H0),
                                        bv_s.rearrange("p (h d) -> p h d", h=H0).unsqueeze(1)
                                        .broadcast_to([P, C, H0, DH]), ALU.add).then_inc(read, 1)
                linked()

                def mask(t, src, bias):
                    linked()
                    link(nc.vector.memset(waited[:], 0.0))
                    nc.vector.tensor_tensor_reduce(out=masked[:, t % 2, :], in0=src, in1=bias, scale=-1.0, scalar=BIG,
                                                   op0=ALU.add, op1=ALU.min, accum_out=negmax[:, t:t + 1])\
                        .then_inc(masked_done, 1)

                def evacuate(t, buf):
                    dve.wait_ge(turned, START + b * NT + t + 1)
                    _l, h, c = TILES[t]
                    nc.vector.tensor_copy(probsT[:, buf, h % 4, :, c * P:(c + 1) * P],
                                          tr[t % 2].rearrange("p (c i) -> p c i", c=C)).then_inc(probsT_dve, 1)

                n0 = len(TILES0)
                for t in range(n0 + 2):
                    if t < n0:
                        dve.wait_ge(scores_done, b * len(SCORES) + t + 1)
                        dve.wait_ge(exp_done, before(b, NT, t))
                        mask(t, scores[t % 2][:], bias0[:, TILES0[t][2], :])
                    if t >= 2 and (t - 2) % 2 == 1:
                        evacuate(t - 2, (t - 2) // 16)
                for g in range(G0):
                    w, read = take(f"ctx{g}")
                    w4 = w.rearrange("p (c h k) -> p c h k", c=C, h=4)
                    link(nc.vector.reciprocal(rden0[:, g, :, :], w4[:, :, :, DH]))
                    linked()
                    nc.vector.tensor_tensor(ctxn[:, :, 4 * g:4 * g + 4, :], w4[:, :, :, 0:DH],
                                            rden0[:, g, :, :].unsqueeze(3).broadcast_to([P, C, 4, DH]), ALU.mult)\
                        .then_inc(read, 1)
                w, read = take("wo")
                dve.wait_ge(x_loaded, b * 16 + 16)
                nc.vector.tensor_tensor(flat(t_s), w[:], flat(x_s), ALU.add).then_inc(read, 1)
                dve.wait_ge(*out_of(b, "wo"))
                link(nc.vector.tensor_tensor(u_s[:], t_s[:], each_chunk(bo_s), ALU.add))
                layernorm(0, u_s, x1, ln1g_s, ln1b_s)
                dve.wait_ge(ln_out, b * LN + 1)
                w, read = take("down")
                nc.vector.tensor_tensor(flat(t_s), w[:], flat(x1), ALU.add).then_inc(read, 1)
                dve.wait_ge(*out_of(b, "down"))
                link(nc.vector.tensor_tensor(u_s[:], t_s[:], each_chunk(b2_s), ALU.add))
                layernorm(1, u_s, x2, ln2g_s, ln2b_s)
                dve.wait_ge(ln_out, b * LN + 2)
                nc.vector.tensor_tensor(flat(t_s), flat(x_s), flat(x2), ALU.add).then_inc(x_used, 1)
                dve.wait_ge(x_used, START + b + 1)
                layernorm(2, t_s, y0)
                for c in range(C):
                    w, read = take(f"yw{c}")
                    dve.wait_ge(yhi, b * C + c + 1)
                    dve.wait_ge(ylo, START + b * C + c)
                    nc.vector.tensor_tensor(yrest[:], w[:], ysplit[:, c, 0, :], ALU.subtract).then_inc(read, 1)
                    dve.wait_ge(*out_of(b, f"yw{c}"))
                    dve.wait_ge(ymid, b * C + c + 1)
                    nc.vector.tensor_tensor(ysplit[:, c, 2, :], yrest[:], ysplit[:, c, 1, :], ALU.subtract)\
                        .then_inc(ylo, 1)
                w, read = take("relT")
                dve.wait_ge(ln_out, b * LN + 3)
                nc.vector.tensor_tensor(flat(t_s), w[:], flat(y0), ALU.add).then_inc(read, 1)
                dve.wait_ge(*out_of(b, "relT"))
                layernorm(3, t_s, y1)

                def attend(first, tiles, k0, bias, buf):
                    for t in range(len(tiles) + 2):
                        if t < len(tiles):
                            _l, h, c = tiles[t]
                            dve.wait_ge(low_done, b * len(TILES2 + TILES3) + first - n0 + t + 1)
                            dve.wait_ge(exp_done, START + b * NT + first + max(t - 1, 0))
                            link(nc.vector.scalar_tensor_tensor(
                                leaky[:, t % 2, :], targets[:, SCORES.index(tiles[t][:2]) % 2, :],
                                s_c[:, c, k0 + h:k0 + h + 1], low[:, t % 2, :], ALU.add, ALU.max))
                            mask(first + t, leaky[:, t % 2, :], bias[:, c, :])
                        if t >= 2 and (t - 2) % 2 == 1:
                            evacuate(first + t - 2, buf)

                w, read = take("s2")
                link(nc.vector.tensor_copy(s_c[:, :, 0], w[:, 0:C]))
                linked()
                nc.vector.tensor_scalar(s_low[:, :, 0], w[:, 0:C], ALPHA, None, ALU.mult).then_inc(read, 1)
                attend(n0, TILES2, 0, bias2, 0)
                dve.wait_ge(exp_done, START + b * NT + n0 + C)
                link(nc.vector.reciprocal(rden[:, 0:C], den[:, n0:n0 + C]))
                linked()
                w, read = take("pv2")
                dve.wait_ge(ln_out, b * LN + 4)
                for c in range(C):
                    ins = nc.vector.scalar_tensor_tensor(t_s[:, c, :], w[:, c * P:(c + 1) * P], rden[:, c:c + 1],
                                                         y1[:, c, :], ALU.mult, ALU.add)
                    if c < C - 1:
                        link(ins)
                ins.then_inc(read, 1)
                dve.wait_ge(*out_of(b, "pv2"))
                layernorm(4, t_s, y2)
                w, read = take("h3")
                nc.vector.tensor_tensor(h3[:], chunks(w), each_chunk(b3r_s), ALU.add).then_inc(read, 1)
                w, read = take("s3")
                link(nc.vector.tensor_tensor(s_c[:, :, 1:1 + H3], w[:, 0:C * H3].rearrange("p (c h) -> p c h", h=H3),
                                             c3s[:].unsqueeze(1).broadcast_to([P, C, H3]), ALU.add))
                linked()
                nc.vector.tensor_scalar(s_low[:, :, 1:1 + H3], s_c[:, :, 1:1 + H3], ALPHA, None, ALU.mult)\
                    .then_inc(read, 1)
                attend(n0 + C, TILES3, 1, bias3, 1)
                dve.wait_ge(exp_done, START + b * NT + NT)
                link(nc.vector.reciprocal(rden[:, C:C + C * H3], den[:, n0 + C:NT]))
                linked()
                w, read = take("pv3")
                nc.vector.tensor_tensor(u_s.rearrange("p c (h k) -> p c h k", h=H3),
                                        w.rearrange("p (c h k) -> p c h k", c=C, h=H3),
                                        rden[:, C:C + C * H3].rearrange("p (h c) -> p c h", h=H3)
                                        .unsqueeze(3).broadcast_to([P, C, H3, DC]), ALU.mult).then_inc(read, 1)
                dve.wait_ge(*out_of(b, "pv3"))
                dve.wait_ge(ln_out, b * LN + 5)
                link(nc.vector.tensor_tensor(flat(t_s), flat(u_s), flat(y2), ALU.add))
                dve.wait_ge(y3_free, START + b)
                layernorm(5, t_s, y3)
                dve.wait_ge(ln_out, b * LN + LN)
                linked()


def heads_padded(w):
    rows = w.reshape(G0, 4, DH, -1)
    padded = np.zeros((G0, 4, 32, rows.shape[-1]), w.dtype)
    padded[:, :, :DH] = rows
    return padded.reshape(G0, P, -1)


def kernel(**inputs):
    import concourse.bacc as bacc
    from concourse.bass_utils import run_bass_kernel_spmd

    v = {k: np.asarray(a) for k, a in inputs.items()}
    wqkv, bqkv = v["L0_gnn_Wqkv"], v["L0_gnn_bqkv"]

    def rows(a):
        return np.broadcast_to(a, (P, a.size))

    a3 = v["L3_gnn_a"]
    a3_blocks = np.zeros((P, 2 * H3), a3.dtype)
    for h in range(H3):
        a3_blocks[h * DC:(h + 1) * DC, h] = a3[h, :DC]
        a3_blocks[h * DC:(h + 1) * DC, H3 + h] = a3[h, DC:]
    arrays = {
        "x": v["x"], "xT": v["x"].transpose(0, 2, 1), "adj": v["adj"], "adjT": v["adj"].transpose(0, 2, 1),
        "wqT": heads_padded(wqkv[:D]).transpose(2, 0, 1), "wkT": heads_padded(wqkv[D:2 * D]).transpose(2, 0, 1),
        "wvT": wqkv[2 * D:].T, "bq": heads_padded(bqkv[:D, None])[:, :, 0].T,
        "bk": heads_padded(bqkv[D:2 * D, None])[:, :, 0].T, "bv": rows(bqkv[2 * D:]),
        "woT": v["L0_gnn_Wo"].T, "bo": rows(v["L0_gnn_bo"]), "w1T": v["L0_gnn_W1"].T,
        "b1": v["L0_gnn_b1"].reshape(F, P).T, "w2T": v["L0_gnn_W2"].T.reshape(F, P, D).transpose(1, 0, 2),
        "b2": rows(v["L0_gnn_b2"]), "ln1g": rows(v["L0_gnn_ln1_g"]), "ln1b": rows(v["L0_gnn_ln1_b"]),
        "ln2g": rows(v["L0_gnn_ln2_g"]), "ln2b": rows(v["L0_gnn_ln2_b"]),
        "rel_w": v["L1_gnn_weight"].transpose(1, 0, 2).reshape(D, R * D), "rel_b": v["L1_gnn_bias"][:, None],
        "w2g": v["L2_gnn_W"], "w2gT": v["L2_gnn_W"].T, "a2g": v["L2_gnn_a"].reshape(2, D).T,
        "w3T": v["L3_gnn_W"].T, "w3": v["L3_gnn_W"], "b3c": v["L3_gnn_b"][:, None], "b3r": rows(v["L3_gnn_b"]),
        "a3": a3_blocks,
    }
    nc = bacc.Bacc("TRN2", target_bir_lowering=False, num_devices=1)
    data, args = {}, []
    for name, a in arrays.items():
        data[f"{name}_in"] = np.ascontiguousarray(a)
        args.append(nc.dram_tensor(f"{name}_in", a.shape, mybir.dt.from_np(a.dtype), kind="ExternalInput").ap())
    args.append(nc.dram_tensor("out", v["x"].shape, mybir.dt.float32, kind="ExternalOutput").ap())
    build(nc, *args)
    return run_bass_kernel_spmd(nc, [data], core_ids=[0]).results[0]["out"]
```

```python
import numpy as np
import concourse.bass as bass
from concourse import mybir
from contextlib import ExitStack

B, N, D = 16, 512, 128
P = 128
C = N // P
H0, DH = 8, 16
G0 = 2
DFF = 512
F = DFF // P
R = 4
H3, DC = 4, 32
EPS = 1e-5
ALPHA = 0.2
NEG_INF = -9000000000000000.0
NEG_L0 = -1.0e30
BIG = 3.0e38
START = 1
SCALE = float(DH) ** -0.5

WORK = (["q", "k", "v", "ctx0", "ctx1", "ctxT", "wo", "x1T"] + [f"up{f}" for f in range(F)]
        + ["down", "y0T"] + [f"yw{c}" for c in range(C)] + ["rel", "relT", "y1T", "wh", "s2", "pv2", "y2T", "h3",
                                                           "s3", "pv3"])
TILES0 = [(0, h, c) for h in range(H0) for c in range(C)]
TILES2 = [(2, 0, c) for c in range(C)]
TILES3 = [(3, h, c) for h in range(H3) for c in range(C)]
TILES = TILES0 + TILES2 + TILES3
SCORES = TILES0 + [(2, 0)] + [(3, h) for h in range(H3)]
LN = 6


def build(nc, x, xT, adj, adjT, wqT, wkT, wvT, bq, bk, bv, woT, bo, w1T, b1, w2T, b2, ln1g, ln1b, ln2g, ln2b,
          rel_w, rel_b, w2g, w2gT, a2g, w3T, w3, b3c, b3r, a3, out):
    f32, bf16, i32 = mybir.dt.float32, mybir.dt.bfloat16, mybir.dt.int32
    ALU, ACT = mybir.AluOpType, mybir.ActivationFunctionType

    with ExitStack() as ctx:
        def sb(name, shape, dt=f32):
            return ctx.enter_context(nc.sbuf_tensor(name, shape, dt))

        def sem(name):
            return ctx.enter_context(nc.semaphore(name))

        def bank(name, shape=(P, 512)):
            return ctx.enter_context(nc.psum_tensor(name, list(shape), f32))

        wq_s, wk_s = sb("wq_s", [P, P]), sb("wk_s", [P, P])
        bq_s, bk_s = sb("bq_s", [P, 1]), sb("bk_s", [P, 1])
        wv_s, bv_s = sb("wv_s", [P, P]), sb("bv_s", [P, P])
        wo_s, bo_s = sb("wo_s", [P, P]), sb("bo_s", [P, P])
        w1_s, b1_s = sb("w1_s", [P, DFF]), sb("b1_s", [P, F])
        w2_s, b2_s = sb("w2_s", [P, F, P]), sb("b2_s", [P, P])
        ln1g_s, ln1b_s = sb("ln1g_s", [P, P]), sb("ln1b_s", [P, P])
        ln2g_s, ln2b_s = sb("ln2g_s", [P, P]), sb("ln2b_s", [P, P])
        relw_s, relb_s = sb("relw_s", [P, R * P]), sb("relb_s", [P, 1])
        w2g_s, w2gT_s, a2_s = sb("w2g_s", [P, P]), sb("w2gT_s", [P, P]), sb("a2_s", [P, 2])
        w3T_s, w3_s = sb("w3T_s", [P, P]), sb("w3_s", [P, P])
        b3c_s, b3r_s, a3_s = sb("b3c_s", [P, 1]), sb("b3r_s", [P, P]), sb("a3_s", [P, 2 * H3])
        LOADS = [(wq_s, wqT), (wk_s, wkT), (bq_s, bq), (bk_s, bk), (wv_s, wvT), (bv_s, bv), (wo_s, woT), (bo_s, bo),
                 (w1_s, w1T), (b1_s, b1), (w2_s, w2T), (b2_s, b2), (ln1g_s, ln1g), (ln1b_s, ln1b), (ln2g_s, ln2g),
                 (ln2b_s, ln2b), (relw_s, rel_w), (relb_s, rel_b), (w2g_s, w2g), (w2gT_s, w2gT), (a2_s, a2g),
                 (w3T_s, w3T), (w3_s, w3), (b3c_s, b3c), (b3r_s, b3r), (a3_s, a3)]
        ident = sb("ident", [P, P])
        offdiag = sb("offdiag", [P, C, 512], bf16)
        half_neg = sb("half_neg", [P, C])
        b3w = sb("b3w", [P, P])
        wa_s = sb("wa_s", [P, 2 + 2 * H3])
        wd_s = sb("wd_s", [P, 1 + H3, P])
        c3 = sb("c3", [P, 2 * H3])
        c3s = sb("c3s", [P, H3])

        xT_s, x_s = sb("xT_s", [P, 512]), sb("x_s", [P, C, P])
        adj_s, adjT_s = sb("adj_s", [P, C, 512], i32), sb("adjT_s", [P, C, 512], i32)
        bias0, bias2, bias3 = (sb(f"bias{k}", [P, C, 512], bf16) for k in (0, 2, 3))
        relT = sb("relT", [P, R, C, 512], bf16)
        qT, kT = sb("qT", [P, 512]), sb("kT", [P, 512])
        bqs = sb("bqs", [P, 1])
        head_rows = sb("head_rows", [P, H0])
        V = sb("V", [P, C * H0, 32])
        masked = sb("masked", [P, 2, 512])
        probs = sb("probs", [P, 2, 512])
        probsT_flat = sb("probsT", [P, 2 * 4 * C * 512])
        probsT = probsT_flat.rearrange("p (u h c i) -> p u h c i", u=2, h=4, c=C)
        leaky = sb("leaky", [P, 2, 512])
        aux = sb("aux", [P, 4, 512])
        targets_line = sb("targets_line", [P, 2, 512])
        qh = aux
        targets, line = aux[:, 0:2, :], aux[:, 2:4, :]
        negmax, den, rden = (sb(n, [P, len(TILES)]) for n in ("negmax", "den", "rden"))
        ctx_s = sb("ctx_s", [P, G0, 512])
        rden0 = sb("rden0", [P, G0, C, 4])
        ctxn, ctxnT = sb("ctxn", [P, C, H0, DH]), sb("ctxnT", [P, 512])
        waited = sb("waited", [P, 8])
        t_s, u_s = sb("t_s", [P, C, P]), sb("u_s", [P, C, P])
        stats, mv = sb("stats", [P, C, 6]), sb("mv", [P, C, 2])
        vare, rstd = sb("vare", [P, C]), sb("rstd", [P, C])
        x1, x1T, hT = sb("x1", [P, C, P]), sb("x1T", [P, 512]), sb("hT", [P, F, 512])
        y0T = y1T = y2T = x1T
        x2 = sb("x2", [P, C, P])
        y0 = sb("y0", [P, C, P])
        yrest = leaky
        ysplit = probsT_flat[:, C * 512:C * 512 + C * 3 * R * P // 2].bitcast(bf16)\
            .rearrange("p (c s n) -> p c s n", c=C, s=3)
        adjmax = ysplit[:, :, 0, :]
        relo = pv3_s = ctxnT
        y1 = sb("y1", [P, C, P])
        wh = sb("wh", [P, C, P])
        s_c = sb("s_c", [P, C, 1 + H3])
        y2 = sb("y2", [P, C, P])
        h3 = wh
        y3 = sb("y3", [P, C, P])

        scores = [bank(f"scores_ps{k}") for k in range(2)]
        tr = [bank(f"tr_ps{k}") for k in range(2)]
        acc = bank("acc_ps")
        work = [bank(f"work_ps{k}") for k in range(3)]

        weights_loaded = sem("weights_loaded")
        pool_const, dve_const, prep_ps, prep_sb = (sem(n) for n in ("pool_const", "dve_const", "prep_ps", "prep_sb"))
        xT_loaded, x_loaded, adj_loaded = sem("xT_loaded"), sem("x_loaded"), sem("adj_loaded")
        masks_ready, x_used = sem("masks_ready"), sem("x_used")
        qh_ready = sem("qh_ready")
        work_done = sem("work_done")
        work_out = [sem(f"work_out{k}") for k in range(3)]
        scores_done = sem("scores_done")
        d_copied = sem("d_copied")
        line_done = sem("line_done")
        masked_done = sem("masked_done")
        exp_done = sem("exp_done")
        turned = sem("turned")
        probsT_act, probsT_dve = sem("probsT_act"), sem("probsT_dve")
        acc_done, acc_out = sem("acc_done"), sem("acc_out")
        ctxn_ready = sem("ctxn_ready")
        ln_var, ln_rstd, ln_out = sem("ln_var"), sem("ln_rstd"), sem("ln_out")
        yhi, ymid, ylo = sem("yhi"), sem("ymid"), sem("ylo")
        stored, y3_free = sem("stored"), sem("y3_free")
        dve_chain = sem("dve_chain")

        STARTED = [masks_ready, x_used, *work_out, masked_done, exp_done, turned, probsT_act, probsT_dve, acc_out,
                   ylo, d_copied, y3_free]

        NT, NW = len(TILES), len(WORK)

        def uses(b, name):
            n = WORK.index(name)
            return work_out[n % 3], START + b * len(range(n % 3, NW, 3)) + n // 3

        def out_of(b, name):
            s, n = uses(b, name)
            return s, n + 1

        def before(b, total, n, slots=2):
            return START + b * total + max(n - slots + 1, 0)

        block = ctx.enter_context(nc.Block())

        def flat(t):
            return t.rearrange("p c d -> p (c d)")

        def chunks(t):
            return t.rearrange("p (c d) -> p c d", c=C)

        def each_chunk(row):
            return row[:].unsqueeze(1).broadcast_to([P, C, P])

        @block.sync
        def _(sp):
            for dst, src in LOADS:
                sp.dma_start(dst[:], src).then_inc(weights_loaded, 16)
            with sp.Fori(0, B) as b:
                sp.wait_ge(masks_ready, START + b)
                sp.dma_start(adj_s[:], adj[b].rearrange("(c p) j -> p c j", p=P)).then_inc(adj_loaded, 16)
                sp.dma_start(adjT_s[:], adjT[b].rearrange("(c p) j -> p c j", p=P)).then_inc(adj_loaded, 16)
                sp.wait_ge(x_used, START + b)
                sp.dma_start(xT_s[:], xT[b]).then_inc(xT_loaded, 16)
                sp.dma_start(x_s[:], x[b].rearrange("(c p) d -> p c d", p=P)).then_inc(x_loaded, 16)
            sp.wait_ge(masks_ready, START + B)
            sp.dma_start(adj_s[:], adj[0].rearrange("(c p) j -> p c j", p=P)).then_inc(adj_loaded, 16)
            sp.dma_start(adjT_s[:], adjT[0].rearrange("(c p) j -> p c j", p=P)).then_inc(adj_loaded, 16)
            sp.wait_ge(stored, B * 16)

        @block.gpsimd
        def _(pool):
            for s in STARTED:
                nc.gpsimd.sem_inc(s, START)
            nc.gpsimd.memset(ident[:], 0.0).then_inc(pool_const, 1)
            nc.gpsimd.memset(offdiag[:], NEG_L0).then_inc(pool_const, 1)
            nc.gpsimd.memset(half_neg[:], -0.5).then_inc(pool_const, 1)
            pool.wait_ge(pool_const, 3)
            nc.gpsimd.affine_select(out=ident[:], in_=ident[:], compare_op=ALU.not_equal, fill=1.0, base=0,
                                    pattern=[[-1, P]], channel_multiplier=1).then_inc(pool_const, 1)
            nc.gpsimd.affine_select(out=offdiag[:], in_=offdiag[:], compare_op=ALU.not_equal, fill=0.0, base=0,
                                    pattern=[[P, C], [-1, 512]], channel_multiplier=1).then_inc(pool_const, 1)
            nc.gpsimd.memset(head_rows[:], 1.0).then_inc(pool_const, 1)
            pool.wait_ge(pool_const, 6)
            nc.gpsimd.affine_select(out=head_rows[:], in_=head_rows[:], compare_op=ALU.is_ge, fill=0.0, base=0,
                                    pattern=[[-DH, H0]], channel_multiplier=1).then_inc(pool_const, 1)
            pool.wait_ge(pool_const, 7)
            nc.gpsimd.affine_select(out=head_rows[:], in_=head_rows[:], compare_op=ALU.is_ge, fill=0.0, base=DH - 1,
                                    pattern=[[DH, H0]], channel_multiplier=-1).then_inc(pool_const, 1)
            pool.wait_ge(pool_const, 8)

            def heads(b):
                pool.wait_ge(*out_of(b, "q"))
                for h in range(H0):
                    if h >= 4:
                        pool.wait_ge(scores_done, b * len(SCORES) + C * (h - 3))
                    nc.gpsimd.tensor_tensor(qh[:, h % 4, :], qT[:], head_rows[:, h:h + 1].broadcast_to([P, 512]),
                                            ALU.mult).then_inc(qh_ready, 1)

            def power(b, n):
                pool.wait_ge(ln_var, b * LN + n + 1)
                nc.gpsimd.tensor_tensor(rstd[:], vare[:], half_neg[:], ALU.pow).then_inc(ln_rstd, 1)

            def lines(b, tiles, first, bias):
                pool.wait_ge(masks_ready, START + b + 1)
                for t, (layer, h, c) in enumerate(tiles):
                    n = SCORES.index((layer, h)) - len(TILES0)
                    pool.wait_ge(d_copied, START + b * (1 + H3) + n + 1)
                    pool.wait_ge(masked_done, START + b * NT + first + max(t - 1, 0))
                    nc.gpsimd.tensor_tensor(line[:, t % 2, :], targets_line[:, n % 2, :], bias[:, c, :], ALU.add)\
                        .then_inc(line_done, 1)

            def layers(b):
                for n in range(4):
                    power(b, n)
                lines(b, TILES2, len(TILES0), bias2)
                power(b, 4)
                lines(b, TILES3, len(TILES0) + C, bias3)
                power(b, 5)

            def store(b):
                pool.wait_ge(ln_out, b * LN + LN)
                pool.dma_start(out[b].rearrange("(c p) d -> p c d", p=P), y3[:]).then_inc(stored, 16)

            heads(0)
            with pool.Fori(0, B - 1) as b:
                layers(b)
                store(b)
                heads(b + 1)
                pool.wait_ge(stored, b * 16 + 16)
                nc.gpsimd.sem_inc(y3_free, 1)
            layers(B - 1)
            store(B - 1)

        @block.tensor
        def _(pe):
            pe.wait_ge(weights_loaded, 16 * len(LOADS))
            pe.wait_ge(dve_const, 3)
            pe.wait_ge(pool_const, 5)
            nc.tensor.matmul(work[0][:, 0:2], w2gT_s[:], a2_s[:], start=True, stop=True)
            nc.tensor.matmul(work[0][:, 2:2 + 2 * H3], w3_s[:], a3_s[:], start=True, stop=True)
            nc.tensor.matmul(work[0][:, 16:16 + 2 * H3], b3w[:], a3_s[:], start=True, stop=True).then_inc(prep_ps, 1)
            pe.wait_ge(prep_sb, 1)

            with pe.Fori(0, B) as b:
                def begin(name):
                    pe.wait_ge(*uses(b, name))
                    return work[WORK.index(name) % 3]

                def transposes(name, src):
                    w = begin(name)
                    for c in range(C):
                        ins = nc.tensor.transpose(w[:, c * P:(c + 1) * P], src(c), ident[:])
                    ins.then_inc(work_done, 1)

                def project(name, xt, w_s):
                    w = begin(name)
                    for c in range(C):
                        ins = nc.tensor.matmul(w[:, c * P:(c + 1) * P], xt[:, c * P:(c + 1) * P], w_s,
                                               start=True, stop=True)
                    ins.then_inc(work_done, 1)

                def turn(t):
                    pe.wait_ge(exp_done, START + b * NT + t + 1)
                    pe.wait_ge((probsT_act, probsT_dve)[t % 2], START + b * (NT // 2) + t // 2)
                    for c in range(C):
                        ins = nc.tensor.transpose(tr[t % 2][:, c * P:(c + 1) * P],
                                                  probs[:, t % 2, c * P:(c + 1) * P], ident[:])
                    ins.then_inc(turned, 1)

                def probsT_full(tiles):
                    pe.wait_ge(probsT_act, START + b * (NT // 2) + tiles // 2)
                    pe.wait_ge(probsT_dve, START + b * (NT // 2) + tiles // 2)

                def pv(n, buf, tiles, value):
                    probsT_full(tiles)
                    pe.wait_ge(acc_out, START + b * 3 + n)
                    for c in range(C):
                        for h in range(4):
                            ins = nc.tensor.matmul(acc[32 * h:32 * h + 32, :], value(c, h), probsT[:, buf, h, c, :],
                                                   start=(c == 0), stop=(c == C - 1), tile_position=(0, 32 * h))
                    ins.then_inc(acc_done, 1)

                pe.wait_ge(xT_loaded, b * 16 + 16)
                for name, w_s in (("q", wq_s), ("k", wk_s)):
                    w = begin(name)
                    nc.tensor.matmul(w[:], w_s[:], xT_s[:], start=True, stop=True).then_inc(work_done, 1)
                project("v", xT_s, wv_s[:])
                for name in ("k", "v"):
                    pe.wait_ge(*out_of(b, name))
                n0 = len(TILES0)
                for t in range(n0 + 2):
                    if t < n0:
                        _l, h, c = TILES0[t]
                        if c == 0:
                            pe.wait_ge(qh_ready, b * H0 + h + 1)
                        pe.wait_ge(masked_done, before(b, NT, t))
                        nc.tensor.matmul(scores[t % 2][:], qh[:, h % 4, c * P:(c + 1) * P], kT[:],
                                         start=True, stop=True).then_inc(scores_done, 1)
                    if t >= 2:
                        turn(t - 2)
                    if t == n0 // 2 + 3:
                        pv(0, 0, n0 // 2, lambda c, h: V[:, c * H0 + h, :])
                pv(1, 1, n0, lambda c, h: V[:, c * H0 + 4 + h, :])
                for g in range(G0):
                    pe.wait_ge(acc_out, START + b * 3 + g + 1)
                    transposes(f"ctx{g}", lambda c: ctx_s[:, g, c * P:(c + 1) * P])
                pe.wait_ge(*out_of(b, "ctx0"))
                pe.wait_ge(*out_of(b, "ctx1"))
                transposes("ctxT", lambda c: ctxn[:, c, :, :].rearrange("p h d -> p (h d)"))
                pe.wait_ge(*out_of(b, "ctxT"))
                project("wo", ctxnT, wo_s[:])
                pe.wait_ge(ln_out, b * LN + 1)
                transposes("x1T", lambda c: x1[:, c, :])
                pe.wait_ge(*out_of(b, "x1T"))
                for f in range(F):
                    w = begin(f"up{f}")
                    nc.tensor.matmul(w[:], w1_s[:, f * P:(f + 1) * P], x1T[:], start=True, stop=True)\
                        .then_inc(work_done, 1)
                for f in range(F):
                    pe.wait_ge(*out_of(b, f"up{f}"))
                w = begin("down")
                for c in range(C):
                    for f in range(F):
                        ins = nc.tensor.matmul(w[:, c * P:(c + 1) * P], hT[:, f, c * P:(c + 1) * P], w2_s[:, f, :],
                                               start=(f == 0), stop=(f == F - 1))
                ins.then_inc(work_done, 1)
                pe.wait_ge(ln_out, b * LN + 3)
                transposes("y0T", lambda c: y0[:, c, :])
                pe.wait_ge(*out_of(b, "y0T"))
                for c in range(C):
                    w = begin(f"yw{c}")
                    nc.tensor.matmul(w[:], y0T[:, c * P:(c + 1) * P], relw_s[:], start=True, stop=True)\
                        .then_inc(work_done, 1)
                w = begin("rel")
                pe.wait_ge(masks_ready, START + b + 1)
                for c in range(C):
                    for part in range(3):
                        if part == 0:
                            pe.wait_ge(yhi, b * C + c + 1)
                        elif part == 1:
                            pe.wait_ge(ymid, b * C + c + 1)
                        else:
                            pe.wait_ge(ylo, START + b * C + c + 1)
                        for r in range(R):
                            ins = nc.tensor.matmul(w[:], ysplit[:, c, part, r * P:(r + 1) * P], relT[:, r, c, :],
                                                   start=(c == part == r == 0),
                                                   stop=(c == C - 1 and part == 2 and r == R - 1))
                ins.then_inc(work_done, 1)
                pe.wait_ge(*out_of(b, "rel"))
                transposes("relT", lambda c: relo[:, c * P:(c + 1) * P])

                def attend(first, tiles, xt, s_name, wh_name, w_s, s_cols):
                    project(wh_name, xt, w_s)
                    w = begin(s_name)
                    k = s_cols.stop - s_cols.start
                    for c in range(C):
                        ins = nc.tensor.matmul(w[:, c * k:c * k + k], xt[:, c * P:(c + 1) * P], wa_s[:, s_cols],
                                               start=True, stop=True)
                    ins.then_inc(work_done, 1)
                    def targets_of(head):
                        n = SCORES.index(tiles[C * head][:2])
                        pe.wait_ge(masked_done, START + b * NT + n0)
                        pe.wait_ge(d_copied, START + b * (1 + H3) + max(n - n0 - 1, 0))
                        nc.tensor.matmul(scores[n % 2][:], wd_s[:, n - n0, :], xt[:], start=True,
                                         stop=True).then_inc(scores_done, 1)

                    targets_of(0)
                    for t in range(len(tiles) + 1):
                        if t % C == 0 and t + C < len(tiles):
                            targets_of(t // C + 1)
                        if t >= 1:
                            turn(first + t - 1)

                pe.wait_ge(ln_out, b * LN + 4)
                transposes("y1T", lambda c: y1[:, c, :])
                pe.wait_ge(*out_of(b, "y1T"))
                attend(n0, TILES2, y1T, "s2", "wh", w2g_s[:], slice(0, 1))
                pe.wait_ge(*out_of(b, "wh"))
                w = begin("pv2")
                probsT_full(n0 + C)
                for c in range(C):
                    for cj in range(C):
                        ins = nc.tensor.matmul(w[:, c * P:(c + 1) * P], probsT[:, 0, 0, cj, c * P:(c + 1) * P],
                                               wh[:, cj, :], start=(cj == 0), stop=(cj == C - 1))
                ins.then_inc(work_done, 1)
                pe.wait_ge(ln_out, b * LN + 5)
                transposes("y2T", lambda c: y2[:, c, :])
                pe.wait_ge(*out_of(b, "y2T"))
                attend(n0 + C, TILES3, y2T, "s3", "h3", w3T_s[:], slice(2, 2 + H3))
                pe.wait_ge(*out_of(b, "h3"))
                pv(2, 1, NT, lambda c, h: h3[:, c, h * DC:(h + 1) * DC])
                pe.wait_ge(acc_out, START + b * 3 + 3)
                transposes("pv3", lambda c: pv3_s[:, c * P:(c + 1) * P])

        @block.scalar
        def _(act):
            act.wait_ge(weights_loaded, 16 * len(LOADS))
            act.wait_ge(prep_sb, 1)
            with act.Fori(0, B) as b:
                def take(name):
                    n = WORK.index(name)
                    act.wait_ge(work_done, b * NW + n + 1)
                    return work[n % 3], work_out[n % 3]

                def copy(name, dst):
                    w, read = take(name)
                    nc.scalar.activation(dst, w[:], ACT.Copy).then_inc(read, 1)

                def exps(t):
                    act.wait_ge(masked_done, START + b * NT + t + 1)
                    act.wait_ge(turned, before(b, NT, t))
                    nc.scalar.activation(probs[:, t % 2, :], masked[:, t % 2, :], ACT.Exp, bias=negmax[:, t:t + 1],
                                         scale=-1.0, accum_out=den[:, t:t + 1]).then_inc(exp_done, 1)

                def evacuate(t, buf):
                    act.wait_ge(turned, START + b * NT + t + 1)
                    _l, h, c = TILES[t]
                    nc.scalar.activation(probsT[:, buf, h % 4, :, c * P:(c + 1) * P],
                                         tr[t % 2].rearrange("p (c i) -> p c i", c=C), ACT.Copy)\
                        .then_inc(probsT_act, 1)

                def sums(n, dst):
                    act.wait_ge(acc_done, b * 3 + n + 1)
                    nc.scalar.activation(dst, acc[:], ACT.Copy).then_inc(acc_out, 1)

                w, read = take("q")
                nc.scalar.activation(qT[:], w[:], ACT.Identity, bias=bqs[:], scale=SCALE).then_inc(read, 1)
                w, read = take("k")
                nc.scalar.activation(kT[:], w[:], ACT.Identity, bias=bk_s[:]).then_inc(read, 1)
                n0 = len(TILES0)
                for t in range(n0 + 2):
                    if t < n0:
                        exps(t)
                    if t >= 2 and t % 2 == 0:
                        evacuate(t - 2, (t - 2) // 16)
                    if t == n0 // 2 + 5:
                        sums(0, ctx_s[:, 0, :])
                sums(1, ctx_s[:, 1, :])
                copy("ctxT", ctxnT[:])
                copy("x1T", x1T[:])
                for f in range(F):
                    w, read = take(f"up{f}")
                    nc.scalar.activation(hT[:, f, :], w[:], ACT.Relu, bias=b1_s[:, f:f + 1]).then_inc(read, 1)
                copy("y0T", y0T[:])
                for c in range(C + 1):
                    if c < C:
                        act.wait_ge(work_done, b * NW + WORK.index(f"yw{c}") + 1)
                        nc.scalar.activation(ysplit[:, c, 0, :], work[WORK.index(f"yw{c}") % 3][:], ACT.Copy)\
                            .then_inc(yhi, 1)
                    if c >= 1:
                        act.wait_ge(*out_of(b, f"yw{c - 1}"))
                        nc.scalar.activation(ysplit[:, c - 1, 1, :], yrest[:, (c - 1) % 2, :], ACT.Copy)\
                            .then_inc(ymid, 1)
                w, read = take("rel")
                nc.scalar.activation(relo[:], w[:], ACT.Identity, bias=relb_s[:]).then_inc(read, 1)

                def attend(first, tiles, k0, buf):
                    def copy_targets(head):
                        n = SCORES.index(tiles[C * head][:2]) - n0
                        act.wait_ge(scores_done, b * len(SCORES) + n0 + n + 1)
                        act.wait_ge(masked_done, START + b * NT + n0 + C * max(n - 1, 0))
                        nc.scalar.activation(targets[:, n % 2, :], scores[n % 2][:], ACT.Copy)
                        nc.scalar.activation(targets_line[:, n % 2, :], scores[n % 2][:], ACT.Copy,
                                             scale=ALPHA / (1 - ALPHA))\
                            .then_inc(d_copied, 1)

                    copy_targets(0)
                    for t in range(len(tiles) + 1):
                        if t % C == 1 and t + C - 1 < len(tiles):
                            copy_targets(t // C + 1)
                        if t < len(tiles):
                            exps(first + t)
                        if t >= 1 and (t - 1) % 2 == 0:
                            evacuate(first + t - 1, buf)

                copy("y1T", y1T[:])
                copy("wh", wh[:])
                attend(n0, TILES2, 0, 0)
                copy("y2T", y2T[:])
                attend(n0 + C, TILES3, 1, 1)
                sums(2, pv3_s[:])

        @block.vector
        def _(dve):
            nc.vector.memset(V[:], 1.0).then_inc(dve_const, 1)
            dve.wait_ge(weights_loaded, 16 * len(LOADS))
            nc.vector.tensor_scalar(bqs[:], bq_s[:], SCALE, None, ALU.mult).then_inc(dve_const, 1)
            nc.vector.tensor_copy(b3w[:], b3c_s[:].broadcast_to([P, P])).then_inc(dve_const, 1)
            dve.wait_ge(prep_ps, 1)
            nc.vector.tensor_copy(wa_s[:], work[0][:, 0:2 + 2 * H3]).then_inc(dve_const, 1)
            nc.vector.tensor_copy(c3[:], work[0][:, 16:16 + 2 * H3]).then_inc(dve_const, 1)
            dve.wait_ge(dve_const, 5)
            nc.vector.tensor_copy(wd_s[:, 0, :], wa_s[:, 1:2].broadcast_to([P, P])).then_inc(dve_const, 1)
            for h in range(H3):
                k = 2 + H3 + h
                nc.vector.tensor_copy(wd_s[:, 1 + h, :], wa_s[:, k:k + 1].broadcast_to([P, P])).then_inc(dve_const, 1)
            nc.vector.tensor_tensor(c3s[:], c3[:, 0:H3], c3[:, H3:2 * H3], ALU.add).then_inc(prep_sb, 1)
            dve.wait_ge(prep_sb, 1)
            dve.wait_ge(pool_const, 5)

            dve.wait_ge(adj_loaded, 32)
            nc.vector.tensor_tensor(adjmax, adj_s[:], adjT_s[:], ALU.max).then_inc(dve_chain, 1)
            dve.wait_ge(dve_chain, 1)
            nc.vector.scalar_tensor_tensor(bias0[:], adjmax, 0.0, offdiag[:], ALU.is_le, ALU.mult)\
                .then_inc(dve_chain, 1)
            dve.wait_ge(dve_chain, 2)

            with dve.Fori(0, B) as b:
                nc.vector.sem_clear(dve_chain)
                chain = [0]

                def link(ins):
                    chain[0] += 1
                    ins.then_inc(dve_chain, 1)

                def linked():
                    dve.wait_ge(dve_chain, chain[0])

                def take(name):
                    n = WORK.index(name)
                    dve.wait_ge(work_done, b * NW + n + 1)
                    return work[n % 3], work_out[n % 3]

                def layernorm(n, src, dst, gain=None, shift=None):
                    linked()
                    for c in range(C):
                        link(nc.vector.bn_stats(stats[:, c, :], src[:, c, :]))
                    linked()
                    for c in range(C):
                        link(nc.vector.bn_aggr(mv[:, c, :], stats[:, c, :]))
                    linked()
                    nc.vector.tensor_scalar(vare[:], mv[:, :, 1], EPS, None, ALU.add).then_inc(ln_var, 1)
                    dve.wait_ge(ln_rstd, b * LN + n + 1)
                    if gain is None:
                        for c in range(C):
                            ins = nc.vector.tensor_scalar(dst[:, c, :], src[:, c, :], mv[:, c, 0:1], rstd[:, c:c + 1],
                                                          ALU.subtract, ALU.mult)
                            if c < C - 1:
                                link(ins)
                        ins.then_inc(ln_out, 1)
                    else:
                        for c in range(C):
                            link(nc.vector.tensor_scalar(dst[:, c, :], src[:, c, :], mv[:, c, 0:1], rstd[:, c:c + 1],
                                                         ALU.subtract, ALU.mult))
                        linked()
                        link(nc.vector.tensor_tensor(dst[:], dst[:], each_chunk(gain), ALU.mult))
                        linked()
                        nc.vector.tensor_tensor(dst[:], dst[:], each_chunk(shift), ALU.add).then_inc(ln_out, 1)

                w, read = take("v")
                nc.vector.tensor_tensor(V.rearrange("p (c h) k -> p c h k", c=C)[:, :, :, 0:DH],
                                        w.rearrange("p (c h d) -> p c h d", c=C, h=H0),
                                        bv_s.rearrange("p (h d) -> p h d", h=H0).unsqueeze(1)
                                        .broadcast_to([P, C, H0, DH]), ALU.add).then_inc(read, 1)
                linked()

                def mask(t, src, bias, scale=1.0):
                    nc.vector.tensor_tensor_reduce(out=masked[:, t % 2, :], in0=src, in1=bias, scale=-scale, scalar=BIG,
                                                   op0=ALU.add, op1=ALU.min, accum_out=negmax[:, t:t + 1])\
                        .then_inc(masked_done, 1)

                def evacuate(t, buf):
                    dve.wait_ge(turned, START + b * NT + t + 1)
                    _l, h, c = TILES[t]
                    nc.vector.tensor_copy(probsT[:, buf, h % 4, :, c * P:(c + 1) * P],
                                          tr[t % 2].rearrange("p (c i) -> p c i", c=C)).then_inc(probsT_dve, 1)

                def other_mask(k):
                    if k == 0:
                        link(nc.vector.tensor_scalar(bias2[:], adj_s[:], 0.0, NEG_INF, ALU.is_le, ALU.mult))
                    elif k == 1:
                        link(nc.vector.tensor_scalar(bias3[:], adj_s[:], 1.0, NEG_INF, ALU.not_equal, ALU.mult))
                    else:
                        ins = nc.vector.tensor_scalar(relT[:, k - 2, :, :], adjT_s[:], float(k - 1), None,
                                                      ALU.is_equal)
                        if k < 1 + R:
                            link(ins)
                        else:
                            ins.then_inc(masks_ready, 1)

                n0 = len(TILES0)
                for t in range(n0 + 3):
                    if t % 3 == 2 and t // 3 < 2 + R:
                        other_mask(t // 3)
                    if t < n0:
                        dve.wait_ge(scores_done, b * len(SCORES) + t + 1)
                        dve.wait_ge(exp_done, before(b, NT, t))
                        link(nc.vector.memset(waited[:, t % 8:t % 8 + 1], 0.0))
                        mask(t, scores[t % 2][:], bias0[:, TILES0[t][2], :])
                    if t >= 3 and (t - 3) % 2 == 1:
                        evacuate(t - 3, (t - 3) // 16)
                for g in range(G0):
                    w, read = take(f"ctx{g}")
                    w4 = w.rearrange("p (c h k) -> p c h k", c=C, h=4)
                    link(nc.vector.reciprocal(rden0[:, g, :, :], w4[:, :, :, DH]))
                    linked()
                    nc.vector.tensor_tensor(ctxn[:, :, 4 * g:4 * g + 4, :], w4[:, :, :, 0:DH],
                                            rden0[:, g, :, :].unsqueeze(3).broadcast_to([P, C, 4, DH]), ALU.mult)\
                        .then_inc(read, 1)
                dve.wait_ge(x_loaded, b * 16 + 16)
                link(nc.vector.tensor_tensor(t_s[:], x_s[:], each_chunk(bo_s), ALU.add))
                linked()
                w, read = take("wo")
                nc.vector.tensor_tensor(flat(u_s), w[:], flat(t_s), ALU.add).then_inc(read, 1)
                dve.wait_ge(*out_of(b, "wo"))
                layernorm(0, u_s, x1, ln1g_s, ln1b_s)
                dve.wait_ge(ln_out, b * LN + 1)
                link(nc.vector.tensor_tensor(t_s[:], x1[:], each_chunk(b2_s), ALU.add))
                linked()
                w, read = take("down")
                nc.vector.tensor_tensor(flat(u_s), w[:], flat(t_s), ALU.add).then_inc(read, 1)
                dve.wait_ge(*out_of(b, "down"))
                layernorm(1, u_s, x2, ln2g_s, ln2b_s)
                dve.wait_ge(ln_out, b * LN + 2)
                nc.vector.tensor_tensor(flat(t_s), flat(x_s), flat(x2), ALU.add).then_inc(x_used, 1)
                dve.wait_ge(x_used, START + b + 1)
                layernorm(2, t_s, y0)
                for c in range(C + 1):
                    if c < C:
                        w, read = take(f"yw{c}")
                        dve.wait_ge(yhi, b * C + c + 1)
                        dve.wait_ge(ylo, before(b, C, c))
                        nc.vector.tensor_tensor(yrest[:, c % 2, :], w[:], ysplit[:, c, 0, :], ALU.subtract)\
                            .then_inc(read, 1)
                    if c >= 1:
                        dve.wait_ge(*out_of(b, f"yw{c - 1}"))
                        dve.wait_ge(ymid, b * C + c)
                        nc.vector.tensor_tensor(ysplit[:, c - 1, 2, :], yrest[:, (c - 1) % 2, :],
                                                ysplit[:, c - 1, 1, :], ALU.subtract).then_inc(ylo, 1)
                w, read = take("relT")
                dve.wait_ge(ln_out, b * LN + 3)
                nc.vector.tensor_tensor(flat(t_s), w[:], flat(y0), ALU.add).then_inc(read, 1)
                dve.wait_ge(*out_of(b, "relT"))
                layernorm(3, t_s, y1)

                def attend(first, tiles, k0, buf):
                    for t in range(len(tiles) + 2):
                        if t < len(tiles):
                            _l, h, c = tiles[t]
                            n = SCORES.index(tiles[t][:2]) - n0
                            dve.wait_ge(d_copied, START + b * (1 + H3) + n + 1)
                            dve.wait_ge(exp_done, START + b * NT + first + max(t - 1, 0))
                            dve.wait_ge(line_done, b * len(TILES2 + TILES3) + first - n0 + t + 1)
                            link(nc.vector.tensor_scalar(leaky[:, t % 2, :], targets[:, n % 2, :],
                                                         s_c[:, c, k0 + h:k0 + h + 1], 0.0, ALU.add, ALU.max))
                            linked()
                            mask(first + t, leaky[:, t % 2, :], line[:, t % 2, :], 1 - ALPHA)
                        if t >= 2 and (t - 2) % 2 == 1:
                            evacuate(first + t - 2, buf)

                w, read = take("s2")
                nc.vector.tensor_copy(s_c[:, :, 0], w[:, 0:C]).then_inc(read, 1)
                dve.wait_ge(*out_of(b, "s2"))
                attend(n0, TILES2, 0, 0)
                dve.wait_ge(exp_done, START + b * NT + n0 + C)
                link(nc.vector.reciprocal(rden[:, 0:C], den[:, n0:n0 + C]))
                linked()
                w, read = take("pv2")
                dve.wait_ge(ln_out, b * LN + 4)
                for c in range(C):
                    ins = nc.vector.scalar_tensor_tensor(t_s[:, c, :], w[:, c * P:(c + 1) * P], rden[:, c:c + 1],
                                                         y1[:, c, :], ALU.mult, ALU.add)
                    if c < C - 1:
                        link(ins)
                ins.then_inc(read, 1)
                dve.wait_ge(*out_of(b, "pv2"))
                layernorm(4, t_s, y2)
                w, read = take("h3")
                nc.vector.tensor_tensor(h3[:], chunks(w), each_chunk(b3r_s), ALU.add).then_inc(read, 1)
                w, read = take("s3")
                nc.vector.tensor_tensor(s_c[:, :, 1:1 + H3], w[:, 0:C * H3].rearrange("p (c h) -> p c h", h=H3),
                                        c3s[:].unsqueeze(1).broadcast_to([P, C, H3]), ALU.add).then_inc(read, 1)
                dve.wait_ge(*out_of(b, "s3"))
                attend(n0 + C, TILES3, 1, 1)
                dve.wait_ge(adj_loaded, b * 32 + 64)
                link(nc.vector.tensor_tensor(adjmax, adj_s[:], adjT_s[:], ALU.max))
                linked()
                link(nc.vector.scalar_tensor_tensor(bias0[:], adjmax, 0.0, offdiag[:], ALU.is_le, ALU.mult))
                dve.wait_ge(exp_done, START + b * NT + NT)
                link(nc.vector.reciprocal(rden[:, C:C + C * H3], den[:, n0 + C:NT]))
                linked()
                w, read = take("pv3")
                nc.vector.tensor_tensor(u_s.rearrange("p c (h k) -> p c h k", h=H3),
                                        w.rearrange("p (c h k) -> p c h k", c=C, h=H3),
                                        rden[:, C:C + C * H3].rearrange("p (h c) -> p c h", h=H3)
                                        .unsqueeze(3).broadcast_to([P, C, H3, DC]), ALU.mult).then_inc(read, 1)
                dve.wait_ge(*out_of(b, "pv3"))
                dve.wait_ge(ln_out, b * LN + 5)
                link(nc.vector.tensor_tensor(flat(t_s), flat(u_s), flat(y2), ALU.add))
                dve.wait_ge(y3_free, START + b)
                layernorm(5, t_s, y3)
                dve.wait_ge(ln_out, b * LN + LN)
                linked()


def kernel(**inputs):
    import concourse.bacc as bacc
    from concourse.bass_utils import run_bass_kernel_spmd

    v = {k: np.asarray(a) for k, a in inputs.items()}
    wqkv, bqkv = v["L0_gnn_Wqkv"], v["L0_gnn_bqkv"]

    def rows(a):
        return np.broadcast_to(a, (P, a.size))

    a3 = v["L3_gnn_a"]
    a3_blocks = np.zeros((P, 2 * H3), a3.dtype)
    for h in range(H3):
        a3_blocks[h * DC:(h + 1) * DC, h] = a3[h, :DC]
        a3_blocks[h * DC:(h + 1) * DC, H3 + h] = a3[h, DC:]
    arrays = {
        "x": v["x"], "xT": v["x"].transpose(0, 2, 1), "adj": v["adj"], "adjT": v["adj"].transpose(0, 2, 1),
        "wqT": wqkv[:D].T, "wkT": wqkv[D:2 * D].T,
        "wvT": wqkv[2 * D:].T, "bq": bqkv[:D, None],
        "bk": bqkv[D:2 * D, None], "bv": rows(bqkv[2 * D:]),
        "woT": v["L0_gnn_Wo"].T, "bo": rows(v["L0_gnn_bo"]), "w1T": v["L0_gnn_W1"].T,
        "b1": v["L0_gnn_b1"].reshape(F, P).T, "w2T": v["L0_gnn_W2"].T.reshape(F, P, D).transpose(1, 0, 2),
        "b2": rows(v["L0_gnn_b2"]), "ln1g": rows(v["L0_gnn_ln1_g"]), "ln1b": rows(v["L0_gnn_ln1_b"]),
        "ln2g": rows(v["L0_gnn_ln2_g"]), "ln2b": rows(v["L0_gnn_ln2_b"]),
        "rel_w": v["L1_gnn_weight"].transpose(1, 0, 2).reshape(D, R * D), "rel_b": v["L1_gnn_bias"][:, None],
        "w2g": v["L2_gnn_W"], "w2gT": v["L2_gnn_W"].T, "a2g": v["L2_gnn_a"].reshape(2, D).T,
        "w3T": v["L3_gnn_W"].T, "w3": v["L3_gnn_W"], "b3c": v["L3_gnn_b"][:, None], "b3r": rows(v["L3_gnn_b"]),
        "a3": a3_blocks,
    }
    nc = bacc.Bacc("TRN2", target_bir_lowering=False, num_devices=1)
    data, args = {}, []
    for name, a in arrays.items():
        data[f"{name}_in"] = np.ascontiguousarray(a)
        args.append(nc.dram_tensor(f"{name}_in", a.shape, mybir.dt.from_np(a.dtype), kind="ExternalInput").ap())
    args.append(nc.dram_tensor("out", v["x"].shape, mybir.dt.float32, kind="ExternalOutput").ap())
    build(nc, *args)
    return run_bass_kernel_spmd(nc, [data], core_ids=[0]).results[0]["out"]
```

```python
import numpy as np
import concourse.bass as bass
from concourse import mybir
from contextlib import ExitStack

B, N, D = 16, 512, 128
P = 128
C = N // P
H0, DH = 8, 16
G0 = 2
DFF = 512
F = DFF // P
R = 4
H3, DC = 4, 32
EPS = 1e-5
ALPHA = 0.2
NEG_INF = -9000000000000000.0
NEG_L0 = -1.0e30
BIG = 3.0e38
START = 1
SCALE = float(DH) ** -0.5

WORK = (["ctx0", "ctx1", "ctxT", "wo", "q", "k", "v", "x1T"] + [f"up{f}" for f in range(F)]
        + ["down", "y0T"] + [f"yw{c}" for c in range(C)] + ["rel", "relT", "y1T", "wh", "s2", "pv2", "y2T", "h3",
                                                           "s3", "pv3"])
TILES0 = [(0, 4 * g + h, c) for g in range(G0) for c in range(C) for h in range(4)]
TILES2 = [(2, 0, c) for c in range(C)]
TILES3 = [(3, h, c) for h in range(H3) for c in range(C)]
TILES = TILES0 + TILES2 + TILES3
SCORES = TILES0 + [(2, 0)] + [(3, h) for h in range(H3)]
DEEP = 4
assert DEEP == F
LN = 6
PRODUCTS = [(0, 0), (0, 1), (1, 0), (1, 1), (0, 2), (2, 0), (1, 2), (2, 1)]
assert len(PRODUCTS) * DH == P


def build(nc, x, xT, adj, adjT, wqT, wkT, wvT, bq, bk, bv, woT, bo, w1T, b1, w2T, b2, ln1g, ln1b, ln2g, ln2b,
          rel_w, rel_b, w2g, w2gT, a2g, w3T, w3, b3c, b3r, a3, parts_d, out):
    f32, bf16, i32 = mybir.dt.float32, mybir.dt.bfloat16, mybir.dt.int32
    ALU, ACT = mybir.AluOpType, mybir.ActivationFunctionType

    with ExitStack() as ctx:
        def sb(name, shape, dt=f32):
            return ctx.enter_context(nc.sbuf_tensor(name, shape, dt))

        def sem(name):
            return ctx.enter_context(nc.semaphore(name))

        def bank(name, shape=(P, 512)):
            return ctx.enter_context(nc.psum_tensor(name, list(shape), f32))

        wq_s, wk_s = sb("wq_s", [P, P]), sb("wk_s", [P, P])
        bq_s, bk_s = sb("bq_s", [P, 1]), sb("bk_s", [P, 1])
        wv_s, bv_s = sb("wv_s", [P, P]), sb("bv_s", [P, P])
        wo_s, bo_s = sb("wo_s", [P, P]), sb("bo_s", [P, P])
        w1_s, b1_s = sb("w1_s", [P, DFF]), sb("b1_s", [P, F])
        w2_s, b2_s = sb("w2_s", [P, F, P]), sb("b2_s", [P, P])
        ln1g_s, ln1b_s = sb("ln1g_s", [P, P]), sb("ln1b_s", [P, P])
        ln2g_s, ln2b_s = sb("ln2g_s", [P, P]), sb("ln2b_s", [P, P])
        relw_s, relb_s = sb("relw_s", [P, R * P]), sb("relb_s", [P, 1])
        w2g_s, w2gT_s, a2_s = sb("w2g_s", [P, P]), sb("w2gT_s", [P, P]), sb("a2_s", [P, 2])
        w3T_s, w3_s = sb("w3T_s", [P, P]), sb("w3_s", [P, P])
        b3c_s, b3r_s, a3_s = sb("b3c_s", [P, 1]), sb("b3r_s", [P, P]), sb("a3_s", [P, 2 * H3])
        LOADS = [(wq_s, wqT), (wk_s, wkT), (bq_s, bq), (bk_s, bk), (wv_s, wvT), (bv_s, bv), (wo_s, woT), (bo_s, bo),
                 (w1_s, w1T), (b1_s, b1), (w2_s, w2T), (b2_s, b2), (ln1g_s, ln1g), (ln1b_s, ln1b), (ln2g_s, ln2g),
                 (ln2b_s, ln2b), (relw_s, rel_w), (relb_s, rel_b), (w2g_s, w2g), (w2gT_s, w2gT), (a2_s, a2g),
                 (w3T_s, w3T), (w3_s, w3), (b3c_s, b3c), (b3r_s, b3r), (a3_s, a3)]
        ident = sb("ident", [P, P])
        offdiag = sb("offdiag", [P, C, 512], bf16)
        pool_waited = sb("pool_waited", [P, 2])
        half_neg, one = sb("half_neg", [P, C]), sb("one", [P, 1])
        b3w = sb("b3w", [P, P])
        wa_s = sb("wa_s", [P, 2 + 2 * H3])
        wd_s = sb("wd_s", [P, 1 + H3, P])
        c3 = sb("c3", [P, 2 * H3])
        c3s = sb("c3s", [P, H3])

        xT_s, x_s = sb("xT_s", [P, 512]), sb("x_s", [P, C, P])
        adj_s, adjT_s = sb("adj_s", [P, C, 512], i32), sb("adjT_s", [P, C, 512], i32)
        bias0, bias2, bias3 = (sb(f"bias{k}", [P, C, 512], bf16) for k in (0, 2, 3))
        relT = sb("relT", [P, R, C, 512], bf16)
        stack = sb("stack", [P, 2, H0, 512], bf16)
        bqs = sb("bqs", [P, 1])
        V = sb("V", [P, C * H0, 32])
        masked = sb("masked", [P, DEEP, 512])
        probs = sb("probs", [P, DEEP, 512])
        probsT_flat = sb("probsT", [P, 2 * 4 * C * 512])
        probsT = probsT_flat.rearrange("p (u h c i) -> p u h c i", u=2, h=4, c=C)
        leaky = sb("leaky", [P, 2, 512])
        aux = sb("aux", [P, 4, 512])
        targets_line = sb("targets_line", [P, 2, 512])
        qk = targets_line
        targets, line = aux[:, 0:2, :], aux[:, 2:4, :]
        parts = aux.rearrange("p a i -> p (a i)")[:, 0:3 * 512].bitcast(bf16).rearrange("p (s q i) -> p s q i", s=3, q=2)
        qk_rest = leaky
        negmax, den, rden = (sb(n, [P, len(TILES)]) for n in ("negmax", "den", "rden"))
        ctx_s = leaky
        rden0 = sb("rden0", [P, G0, C, 4])
        ctxn, ctxnT = sb("ctxn", [P, C, H0, DH]), sb("ctxnT", [P, 512])
        waited = sb("waited", [P, 8])
        t_s, u_s = sb("t_s", [P, C, P]), sb("u_s", [P, C, P])
        stats, mv = sb("stats", [P, C, 6]), sb("mv", [P, C, 2])
        vare, rstd = sb("vare", [P, C]), sb("rstd", [P, C])
        x1, x1T = sb("x1", [P, C, P]), sb("x1T", [P, 512])
        hT = masked
        y0T = y1T = y2T = x1T
        x2 = u_s
        y0 = sb("y0", [P, C, P])
        yrest = leaky
        ysplit = probsT_flat[:, C * 512:C * 512 + C * 3 * R * P // 2].bitcast(bf16)\
            .rearrange("p (c s n) -> p c s n", c=C, s=3)
        adjmax = ysplit[:, :, 0, :]
        relo = pv3_s = ctxnT
        y1 = x1
        wh = sb("wh", [P, C, P])
        s_c = sb("s_c", [P, C, 1 + H3])
        y2 = y0
        h3 = wh
        y3 = sb("y3", [P, C, P])

        scores = [bank(f"scores_ps{k}") for k in range(2)]
        tr = [bank(f"tr_ps{k}") for k in range(2)]
        acc = bank("acc_ps")
        work = [bank(f"work_ps{k}") for k in range(3)]

        weights_loaded = sem("weights_loaded")
        pool_const, dve_const, prep_ps, prep_sb = (sem(n) for n in ("pool_const", "dve_const", "prep_ps", "prep_sb"))
        xT_loaded, x_loaded, adj_loaded = sem("xT_loaded"), sem("x_loaded"), sem("adj_loaded")
        mask3_begun = sem("mask3_begun")
        masks_ready, x_used = sem("masks_ready"), sem("x_used")
        first_ps, first_sb = sem("first_ps"), sem("first_sb")
        split_step = sem("split_step")
        parts_stored, stack_loaded = sem("parts_stored"), sem("stack_loaded")
        work_done = sem("work_done")
        work_out = [sem(f"work_out{k}") for k in range(3)]
        scores_done = sem("scores_done")
        d_copied = sem("d_copied")
        line_done = sem("line_done")
        masked_done = sem("masked_done")
        exp_done = sem("exp_done")
        turned = sem("turned")
        probsT_act, probsT_dve = sem("probsT_act"), sem("probsT_dve")
        acc_done, acc_out = sem("acc_done"), sem("acc_out")
        ctxn_ready = sem("ctxn_ready")
        ln_var, ln_rstd, ln_out = sem("ln_var"), sem("ln_rstd"), sem("ln_out")
        yhi, ymid, ylo = sem("yhi"), sem("ymid"), sem("ylo")
        stored, y3_free = sem("stored"), sem("y3_free")
        dve_chain = sem("dve_chain")

        STARTED = [masks_ready, x_used, *work_out, masked_done, exp_done, turned, probsT_act, probsT_dve, acc_out,
                   ylo, d_copied, y3_free]

        NT, NW = len(TILES), len(WORK)

        def uses(b, name):
            n = WORK.index(name)
            return work_out[n % 3], START + b * len(range(n % 3, NW, 3)) + n // 3

        def out_of(b, name):
            s, n = uses(b, name)
            return s, n + 1

        def before(b, total, n, slots):
            return START + b * total + max(n - slots + 1, 0)

        block = ctx.enter_context(nc.Block())

        def flat(t):
            return t.rearrange("p c d -> p (c d)")

        def chunks(t):
            return t.rearrange("p (c d) -> p c d", c=C)

        def each_chunk(row):
            return row[:].unsqueeze(1).broadcast_to([P, C, P])

        @block.sync
        def _(sp):
            for dst, src in LOADS:
                sp.dma_start(dst[:], src).then_inc(weights_loaded, 16)

            def load_adj(b):
                sp.dma_start(adj_s[:], adj[b].rearrange("(c p) j -> p c j", p=P)).then_inc(adj_loaded, 16)
                sp.dma_start(adjT_s[:], adjT[b].rearrange("(c p) j -> p c j", p=P)).then_inc(adj_loaded, 16)

            def load_x(b):
                sp.dma_start(x_s[:], x[b].rearrange("(c p) d -> p c d", p=P)).then_inc(x_loaded, 16)

            def stack_parts(b):
                sp.wait_ge(split_step, b * 4 + 4)
                sp.dma_start(parts_d, parts[:]).then_inc(parts_stored, 16)
                sp.wait_ge(parts_stored, b * 16 + 16)
                for k, pair in enumerate(PRODUCTS):
                    for side, part in enumerate(pair):
                        sp.dma_start(stack[k * DH:(k + 1) * DH, side, :, :],
                                     parts_d[:, part, side, :].rearrange("(h d) i -> d h i", d=DH))\
                            .then_inc(stack_loaded, 16)

            def load_xT(b):
                sp.dma_start(xT_s[:], xT[b]).then_inc(xT_loaded, 16)

            def ahead(b, following):
                sp.wait_ge(masks_ready, START + b + 1)
                load_adj(following)
                stack_parts(b + 1)

            load_xT(0)
            load_adj(0)
            load_x(0)
            stack_parts(0)
            sp.wait_ge(first_sb, 3)
            load_xT(1)
            with sp.Fori(0, B - 2) as b:
                ahead(b, b + 1)
                sp.wait_ge(x_used, START + b + 1)
                load_x(b + 1)
                load_xT(b + 2)
            ahead(B - 2, B - 1)
            sp.wait_ge(x_used, START + B - 1)
            load_x(B - 1)
            load_xT(0)
            ahead(B - 1, 0)
            sp.wait_ge(stack_loaded, (B + 1) * 16 * 2 * len(PRODUCTS))
            sp.wait_ge(stored, B * 16)

        @block.gpsimd
        def _(pool):
            for s in STARTED:
                nc.gpsimd.sem_inc(s, START)
            nc.gpsimd.memset(ident[:], 0.0).then_inc(pool_const, 1)
            nc.gpsimd.memset(offdiag[:], NEG_L0).then_inc(pool_const, 1)
            nc.gpsimd.memset(half_neg[:], -0.5).then_inc(pool_const, 1)
            pool.wait_ge(pool_const, 3)
            nc.gpsimd.affine_select(out=ident[:], in_=ident[:], compare_op=ALU.not_equal, fill=1.0, base=0,
                                    pattern=[[-1, P]], channel_multiplier=1).then_inc(pool_const, 1)
            nc.gpsimd.affine_select(out=offdiag[:], in_=offdiag[:], compare_op=ALU.not_equal, fill=0.0, base=0,
                                    pattern=[[P, C], [-1, 512]], channel_multiplier=1).then_inc(pool_const, 1)
            nc.gpsimd.memset(one[:], 1.0).then_inc(pool_const, 1)
            pool.wait_ge(pool_const, 6)
            ones = one[:].unsqueeze(1).broadcast_to([P, 2, 512])

            def split(b):
                nc.gpsimd.tensor_tensor(parts[:, 0], qk[:], ones, ALU.mult).then_inc(split_step, 1)
                pool.wait_ge(split_step, b * 4 + 1)
                nc.gpsimd.tensor_tensor(qk_rest[:], qk[:], parts[:, 0], ALU.subtract).then_inc(split_step, 1)
                pool.wait_ge(split_step, b * 4 + 2)
                nc.gpsimd.tensor_tensor(parts[:, 1], qk_rest[:], ones, ALU.mult).then_inc(split_step, 1)
                pool.wait_ge(split_step, b * 4 + 3)
                nc.gpsimd.tensor_tensor(parts[:, 2], qk_rest[:], parts[:, 1], ALU.subtract).then_inc(split_step, 1)

            def power(b, n):
                pool.wait_ge(ln_var, b * LN + n + 1)
                nc.gpsimd.tensor_tensor(rstd[:], vare[:], half_neg[:], ALU.pow).then_inc(ln_rstd, 1)

            def lines(b, tiles, first, bias):
                pool.wait_ge(masks_ready, START + b + 1)
                for t, (layer, h, c) in enumerate(tiles):
                    n = SCORES.index((layer, h)) - len(TILES0)
                    pool.wait_ge(d_copied, START + b * (1 + H3) + n + 1)
                    pool.wait_ge(masked_done, START + b * NT + first + max(t - 1, 0))
                    nc.gpsimd.tensor_tensor(line[:, t % 2, :], targets_line[:, n % 2, :], bias[:, c, :], ALU.add)\
                        .then_inc(line_done, 1)

            def masks(b):
                def small_write(k):
                    nc.gpsimd.tensor_tensor(pool_waited[:, k:k + 1], half_neg[:, 0:1], half_neg[:, 0:1], ALU.add)

                pool.wait_ge(adj_loaded, b * 32 + 32)
                small_write(0)
                nc.gpsimd.tensor_scalar(bias2[:], adj_s[:], 0.0, NEG_INF, ALU.is_le, ALU.mult)
                nc.gpsimd.tensor_scalar(bias3[:], adj_s[:], 1.0, -1.0, ALU.is_equal, ALU.add).then_inc(mask3_begun, 1)
                for r in range(R):
                    nc.gpsimd.tensor_scalar(relT[:, r, :, :], adjT_s[:], float(r + 1), None, ALU.is_equal)
                pool.wait_ge(masked_done, START + b * NT + 1)
                pool.wait_ge(mask3_begun, b + 1)
                small_write(1)
                nc.gpsimd.tensor_scalar(bias3[:], bias3[:], -NEG_INF, None, ALU.mult).then_inc(masks_ready, 1)

            def layers(b):
                masks(b)
                power(b, 0)
                for name in ("q", "k"):
                    pool.wait_ge(*out_of(b, name))
                split(b + 1)
                for n in range(1, 4):
                    power(b, n)
                lines(b, TILES2, len(TILES0), bias2)
                power(b, 4)
                lines(b, TILES3, len(TILES0) + C, bias3)
                power(b, 5)

            def store(b):
                pool.wait_ge(ln_out, b * LN + LN)
                pool.dma_start(out[b].rearrange("(c p) d -> p c d", p=P), y3[:]).then_inc(stored, 16)

            pool.wait_ge(first_sb, 3)
            split(0)
            with pool.Fori(0, B - 1) as b:
                layers(b)
                store(b)
                pool.wait_ge(stored, b * 16 + 16)
                nc.gpsimd.sem_inc(y3_free, 1)
            layers(B - 1)
            store(B - 1)

        @block.tensor
        def _(pe):
            pe.wait_ge(weights_loaded, 16 * len(LOADS))
            pe.wait_ge(dve_const, 3)
            pe.wait_ge(pool_const, 5)
            nc.tensor.matmul(work[0][:, 0:2], w2gT_s[:], a2_s[:], start=True, stop=True)
            nc.tensor.matmul(work[0][:, 2:2 + 2 * H3], w3_s[:], a3_s[:], start=True, stop=True)
            nc.tensor.matmul(work[0][:, 16:16 + 2 * H3], b3w[:], a3_s[:], start=True, stop=True).then_inc(prep_ps, 1)
            pe.wait_ge(prep_sb, 1)

            pe.wait_ge(xT_loaded, 16)
            for w, w_s in zip(scores, (wq_s, wk_s)):
                nc.tensor.matmul(w[:], w_s[:], xT_s[:], start=True, stop=True).then_inc(first_ps, 1)
            for c in range(C):
                ins = nc.tensor.matmul(tr[0][:, c * P:(c + 1) * P], xT_s[:, c * P:(c + 1) * P], wv_s[:],
                                       start=True, stop=True)
            ins.then_inc(first_ps, 1)
            pe.wait_ge(first_sb, 3)

            with pe.Fori(0, B) as b:
                def begin(name):
                    pe.wait_ge(*uses(b, name))
                    return work[WORK.index(name) % 3]

                def transposes(name, src):
                    w = begin(name)
                    for c in range(C):
                        ins = nc.tensor.transpose(w[:, c * P:(c + 1) * P], src(c), ident[:])
                    ins.then_inc(work_done, 1)

                def project(name, xt, w_s):
                    w = begin(name)
                    for c in range(C):
                        ins = nc.tensor.matmul(w[:, c * P:(c + 1) * P], xt[:, c * P:(c + 1) * P], w_s,
                                               start=True, stop=True)
                    ins.then_inc(work_done, 1)

                def turn(t):
                    pe.wait_ge(exp_done, START + b * NT + t + 1)
                    pe.wait_ge((probsT_act, probsT_dve)[t % 2], START + b * (NT // 2) + t // 2)
                    for c in range(C):
                        ins = nc.tensor.transpose(tr[t % 2][:, c * P:(c + 1) * P],
                                                  probs[:, t % DEEP, c * P:(c + 1) * P], ident[:])
                    ins.then_inc(turned, 1)

                def probsT_full(tiles):
                    pe.wait_ge(probsT_act, START + b * (NT // 2) + tiles // 2)
                    pe.wait_ge(probsT_dve, START + b * (NT // 2) + tiles // 2)

                def pv(n, buf, tiles, value):
                    probsT_full(tiles)
                    pe.wait_ge(acc_out, START + b * 3 + n)
                    for c in range(C):
                        for h in range(4):
                            ins = nc.tensor.matmul(acc[32 * h:32 * h + 32, :], value(c, h), probsT[:, buf, h, c, :],
                                                   start=(c == 0), stop=(c == C - 1), tile_position=(0, 32 * h))
                    ins.then_inc(acc_done, 1)

                def pv0(m):
                    g, ci = divmod(m, C)
                    probsT_full(4 * m + 4)
                    if ci == 0:
                        pe.wait_ge(acc_out, START + b * 3 + g)
                    i = slice(ci * P, ci * P + P)
                    for c in range(C):
                        for h in range(4):
                            ins = nc.tensor.matmul(acc[32 * h:32 * h + 32, i], V[:, c * H0 + 4 * g + h, :],
                                                   probsT[:, g, h, c, i], start=(c == 0), stop=(c == C - 1),
                                                   tile_position=(0, 32 * h))
                    if ci == C - 1:
                        ins.then_inc(acc_done, 1)

                pe.wait_ge(stack_loaded, b * 32 * len(PRODUCTS) + 32 * len(PRODUCTS))
                n0 = len(TILES0)
                for t in range(n0 + 3):
                    if t < n0:
                        _l, h, c = TILES0[t]
                        pe.wait_ge(masked_done, before(b, NT, t, 2))
                        nc.tensor.matmul(scores[t % 2][:], stack[:, 0, h, c * P:(c + 1) * P], stack[:, 1, h, :],
                                         start=True, stop=True).then_inc(scores_done, 1)
                    if t >= 3:
                        turn(t - 3)
                    if t >= 8 and t % 4 == 0:
                        pv0(t // 4 - 2)
                pv0(n0 // 4 - 1)
                for g in range(G0):
                    pe.wait_ge(acc_out, START + b * 3 + g + 1)
                    transposes(f"ctx{g}", lambda c: ctx_s[:, g, c * P:(c + 1) * P])
                pe.wait_ge(*out_of(b, "ctx0"))
                pe.wait_ge(*out_of(b, "ctx1"))
                transposes("ctxT", lambda c: ctxn[:, c, :, :].rearrange("p h d -> p (h d)"))
                pe.wait_ge(*out_of(b, "ctxT"))
                project("wo", ctxnT, wo_s[:])
                pe.wait_ge(xT_loaded, b * 16 + 32)
                for name, w_s in (("q", wq_s), ("k", wk_s)):
                    w = begin(name)
                    nc.tensor.matmul(w[:], w_s[:], xT_s[:], start=True, stop=True).then_inc(work_done, 1)
                project("v", xT_s, wv_s[:])
                pe.wait_ge(ln_out, b * LN + 1)
                transposes("x1T", lambda c: x1[:, c, :])
                pe.wait_ge(*out_of(b, "x1T"))
                for f in range(F):
                    w = begin(f"up{f}")
                    nc.tensor.matmul(w[:], w1_s[:, f * P:(f + 1) * P], x1T[:], start=True, stop=True)\
                        .then_inc(work_done, 1)
                for f in range(F):
                    pe.wait_ge(*out_of(b, f"up{f}"))
                w = begin("down")
                for c in range(C):
                    for f in range(F):
                        ins = nc.tensor.matmul(w[:, c * P:(c + 1) * P], hT[:, f, c * P:(c + 1) * P], w2_s[:, f, :],
                                               start=(f == 0), stop=(f == F - 1))
                ins.then_inc(work_done, 1)
                pe.wait_ge(ln_out, b * LN + 3)
                transposes("y0T", lambda c: y0[:, c, :])
                pe.wait_ge(*out_of(b, "y0T"))
                for c in range(C):
                    w = begin(f"yw{c}")
                    nc.tensor.matmul(w[:], y0T[:, c * P:(c + 1) * P], relw_s[:], start=True, stop=True)\
                        .then_inc(work_done, 1)
                w = begin("rel")
                pe.wait_ge(masks_ready, START + b + 1)
                for c in range(C):
                    for part in range(3):
                        if part == 0:
                            pe.wait_ge(yhi, b * C + c + 1)
                        elif part == 1:
                            pe.wait_ge(ymid, b * C + c + 1)
                        else:
                            pe.wait_ge(ylo, START + b * C + c + 1)
                        for r in range(R):
                            ins = nc.tensor.matmul(w[:], ysplit[:, c, part, r * P:(r + 1) * P], relT[:, r, c, :],
                                                   start=(c == part == r == 0),
                                                   stop=(c == C - 1 and part == 2 and r == R - 1))
                ins.then_inc(work_done, 1)
                pe.wait_ge(*out_of(b, "rel"))
                transposes("relT", lambda c: relo[:, c * P:(c + 1) * P])

                def attend(first, tiles, xt, s_name, wh_name, w_s, s_cols):
                    project(wh_name, xt, w_s)
                    w = begin(s_name)
                    k = s_cols.stop - s_cols.start
                    for c in range(C):
                        ins = nc.tensor.matmul(w[:, c * k:c * k + k], xt[:, c * P:(c + 1) * P], wa_s[:, s_cols],
                                               start=True, stop=True)
                    ins.then_inc(work_done, 1)
                    def targets_of(head):
                        n = SCORES.index(tiles[C * head][:2])
                        pe.wait_ge(masked_done, START + b * NT + n0)
                        pe.wait_ge(d_copied, START + b * (1 + H3) + max(n - n0 - 1, 0))
                        nc.tensor.matmul(scores[n % 2][:], wd_s[:, n - n0, :], xt[:], start=True,
                                         stop=True).then_inc(scores_done, 1)

                    targets_of(0)
                    for t in range(len(tiles) + 1):
                        if t % C == 0 and t + C < len(tiles):
                            targets_of(t // C + 1)
                        if t >= 1:
                            turn(first + t - 1)

                pe.wait_ge(ln_out, b * LN + 4)
                transposes("y1T", lambda c: y1[:, c, :])
                pe.wait_ge(*out_of(b, "y1T"))
                attend(n0, TILES2, y1T, "s2", "wh", w2g_s[:], slice(0, 1))
                pe.wait_ge(*out_of(b, "wh"))
                w = begin("pv2")
                probsT_full(n0 + C)
                for c in range(C):
                    for cj in range(C):
                        ins = nc.tensor.matmul(w[:, c * P:(c + 1) * P], probsT[:, 0, 0, cj, c * P:(c + 1) * P],
                                               wh[:, cj, :], start=(cj == 0), stop=(cj == C - 1))
                ins.then_inc(work_done, 1)
                pe.wait_ge(ln_out, b * LN + 5)
                transposes("y2T", lambda c: y2[:, c, :])
                pe.wait_ge(*out_of(b, "y2T"))
                attend(n0 + C, TILES3, y2T, "s3", "h3", w3T_s[:], slice(2, 2 + H3))
                pe.wait_ge(*out_of(b, "h3"))
                pv(2, 1, NT, lambda c, h: h3[:, c, h * DC:(h + 1) * DC])
                pe.wait_ge(acc_out, START + b * 3 + 3)
                transposes("pv3", lambda c: pv3_s[:, c * P:(c + 1) * P])

        @block.scalar
        def _(act):
            act.wait_ge(weights_loaded, 16 * len(LOADS))
            act.wait_ge(prep_sb, 1)

            def q_out(bank, read):
                nc.scalar.activation(qk[:, 0, :], bank[:], ACT.Identity, bias=bqs[:], scale=SCALE).then_inc(read, 1)

            def k_out(bank, read):
                nc.scalar.activation(qk[:, 1, :], bank[:], ACT.Identity, bias=bk_s[:]).then_inc(read, 1)

            act.wait_ge(first_ps, 2)
            q_out(scores[0], first_sb)
            k_out(scores[1], first_sb)
            with act.Fori(0, B) as b:
                def take(name):
                    n = WORK.index(name)
                    act.wait_ge(work_done, b * NW + n + 1)
                    return work[n % 3], work_out[n % 3]

                def copy(name, dst):
                    w, read = take(name)
                    nc.scalar.activation(dst, w[:], ACT.Copy).then_inc(read, 1)

                def exps(t):
                    act.wait_ge(masked_done, START + b * NT + t + 1)
                    act.wait_ge(turned, before(b, NT, t, DEEP))
                    nc.scalar.activation(probs[:, t % DEEP, :], masked[:, t % DEEP, :], ACT.Exp, bias=negmax[:, t:t + 1],
                                         scale=-1.0, accum_out=den[:, t:t + 1]).then_inc(exp_done, 1)

                def evacuate(t, buf):
                    act.wait_ge(turned, START + b * NT + t + 1)
                    _l, h, c = TILES[t]
                    nc.scalar.activation(probsT[:, buf, h % 4, :, c * P:(c + 1) * P],
                                         tr[t % 2].rearrange("p (c i) -> p c i", c=C), ACT.Copy)\
                        .then_inc(probsT_act, 1)

                def sums(n, dst):
                    act.wait_ge(acc_done, b * 3 + n + 1)
                    nc.scalar.activation(dst, acc[:], ACT.Copy).then_inc(acc_out, 1)

                n0 = len(TILES0)
                for t in range(n0 + 3):
                    if t < n0:
                        exps(t)
                    if t >= 3 and (t - 3) % 2 == 0:
                        evacuate(t - 3, (t - 3) // 16)
                    if t == n0 // 2 + 6:
                        sums(0, ctx_s[:, 0, :])
                sums(1, ctx_s[:, 1, :])
                copy("ctxT", ctxnT[:])
                q_out(*take("q"))
                k_out(*take("k"))
                copy("x1T", x1T[:])
                for f in range(F):
                    w, read = take(f"up{f}")
                    nc.scalar.activation(hT[:, f, :], w[:], ACT.Relu, bias=b1_s[:, f:f + 1]).then_inc(read, 1)
                copy("y0T", y0T[:])
                for c in range(C + 1):
                    if c < C:
                        act.wait_ge(work_done, b * NW + WORK.index(f"yw{c}") + 1)
                        nc.scalar.activation(ysplit[:, c, 0, :], work[WORK.index(f"yw{c}") % 3][:], ACT.Copy)\
                            .then_inc(yhi, 1)
                    if c >= 1:
                        act.wait_ge(*out_of(b, f"yw{c - 1}"))
                        nc.scalar.activation(ysplit[:, c - 1, 1, :], yrest[:, (c - 1) % 2, :], ACT.Copy)\
                            .then_inc(ymid, 1)
                w, read = take("rel")
                nc.scalar.activation(relo[:], w[:], ACT.Identity, bias=relb_s[:]).then_inc(read, 1)

                def attend(first, tiles, k0, buf):
                    def copy_targets(head):
                        n = SCORES.index(tiles[C * head][:2]) - n0
                        act.wait_ge(scores_done, b * len(SCORES) + n0 + n + 1)
                        act.wait_ge(masked_done, START + b * NT + n0 + C * max(n - 1, 0))
                        nc.scalar.activation(targets[:, n % 2, :], scores[n % 2][:], ACT.Copy)
                        nc.scalar.activation(targets_line[:, n % 2, :], scores[n % 2][:], ACT.Copy,
                                             scale=ALPHA / (1 - ALPHA))\
                            .then_inc(d_copied, 1)

                    copy_targets(0)
                    for t in range(len(tiles) + 1):
                        if t % C == 1 and t + C - 1 < len(tiles):
                            copy_targets(t // C + 1)
                        if t < len(tiles):
                            exps(first + t)
                        if t >= 1 and (t - 1) % 2 == 0:
                            evacuate(first + t - 1, buf)

                copy("y1T", y1T[:])
                copy("wh", wh[:])
                act.wait_ge(parts_stored, b * 16 + 32)
                attend(n0, TILES2, 0, 0)
                copy("y2T", y2T[:])
                attend(n0 + C, TILES3, 1, 1)
                sums(2, pv3_s[:])

        @block.vector
        def _(dve):
            nc.vector.memset(V[:], 1.0).then_inc(dve_const, 1)
            dve.wait_ge(weights_loaded, 16 * len(LOADS))
            nc.vector.tensor_scalar(bqs[:], bq_s[:], SCALE, None, ALU.mult).then_inc(dve_const, 1)
            nc.vector.tensor_copy(b3w[:], b3c_s[:].broadcast_to([P, P])).then_inc(dve_const, 1)
            dve.wait_ge(prep_ps, 1)
            nc.vector.tensor_copy(wa_s[:], work[0][:, 0:2 + 2 * H3]).then_inc(dve_const, 1)
            nc.vector.tensor_copy(c3[:], work[0][:, 16:16 + 2 * H3]).then_inc(dve_const, 1)
            dve.wait_ge(dve_const, 5)
            nc.vector.tensor_copy(wd_s[:, 0, :], wa_s[:, 1:2].broadcast_to([P, P])).then_inc(dve_const, 1)
            for h in range(H3):
                k = 2 + H3 + h
                nc.vector.tensor_copy(wd_s[:, 1 + h, :], wa_s[:, k:k + 1].broadcast_to([P, P])).then_inc(dve_const, 1)
            nc.vector.tensor_tensor(c3s[:], c3[:, 0:H3], c3[:, H3:2 * H3], ALU.add).then_inc(prep_sb, 1)
            dve.wait_ge(prep_sb, 1)
            dve.wait_ge(pool_const, 5)

            def v_out(bank, read):
                nc.vector.tensor_tensor(V.rearrange("p (c h) k -> p c h k", c=C)[:, :, :, 0:DH],
                                        bank.rearrange("p (c h d) -> p c h d", c=C, h=H0),
                                        bv_s.rearrange("p (h d) -> p h d", h=H0).unsqueeze(1)
                                        .broadcast_to([P, C, H0, DH]), ALU.add).then_inc(read, 1)

            dve.wait_ge(first_ps, 3)
            v_out(tr[0], first_sb)

            dve.wait_ge(adj_loaded, 32)
            nc.vector.tensor_tensor(adjmax, adj_s[:], adjT_s[:], ALU.max).then_inc(dve_chain, 1)
            dve.wait_ge(dve_chain, 1)
            nc.vector.scalar_tensor_tensor(bias0[:], adjmax, 0.0, offdiag[:], ALU.is_le, ALU.mult)\
                .then_inc(dve_chain, 1)
            dve.wait_ge(dve_chain, 2)

            with dve.Fori(0, B) as b:
                nc.vector.sem_clear(dve_chain)
                chain = [0]

                def link(ins):
                    chain[0] += 1
                    ins.then_inc(dve_chain, 1)

                def linked():
                    dve.wait_ge(dve_chain, chain[0])

                def take(name):
                    n = WORK.index(name)
                    dve.wait_ge(work_done, b * NW + n + 1)
                    return work[n % 3], work_out[n % 3]

                def layernorm(n, src, dst, gain=None, shift=None):
                    linked()
                    for c in range(C):
                        link(nc.vector.bn_stats(stats[:, c, :], src[:, c, :]))
                    linked()
                    for c in range(C):
                        link(nc.vector.bn_aggr(mv[:, c, :], stats[:, c, :]))
                    linked()
                    nc.vector.tensor_scalar(vare[:], mv[:, :, 1], EPS, None, ALU.add).then_inc(ln_var, 1)
                    dve.wait_ge(ln_rstd, b * LN + n + 1)
                    if gain is None:
                        for c in range(C):
                            ins = nc.vector.tensor_scalar(dst[:, c, :], src[:, c, :], mv[:, c, 0:1], rstd[:, c:c + 1],
                                                          ALU.subtract, ALU.mult)
                            if c < C - 1:
                                link(ins)
                        ins.then_inc(ln_out, 1)
                    else:
                        for c in range(C):
                            link(nc.vector.tensor_scalar(dst[:, c, :], src[:, c, :], mv[:, c, 0:1], rstd[:, c:c + 1],
                                                         ALU.subtract, ALU.mult))
                        linked()
                        link(nc.vector.tensor_tensor(dst[:], dst[:], each_chunk(gain), ALU.mult))
                        linked()
                        nc.vector.tensor_tensor(dst[:], dst[:], each_chunk(shift), ALU.add).then_inc(ln_out, 1)

                def mask(t, src, bias, scale=1.0):
                    nc.vector.tensor_tensor_reduce(out=masked[:, t % DEEP, :], in0=src, in1=bias, scale=-scale, scalar=BIG,
                                                   op0=ALU.add, op1=ALU.min, accum_out=negmax[:, t:t + 1])\
                        .then_inc(masked_done, 1)

                def evacuate(t, buf):
                    dve.wait_ge(turned, START + b * NT + t + 1)
                    _l, h, c = TILES[t]
                    nc.vector.tensor_copy(probsT[:, buf, h % 4, :, c * P:(c + 1) * P],
                                          tr[t % 2].rearrange("p (c i) -> p c i", c=C)).then_inc(probsT_dve, 1)

                n0 = len(TILES0)
                for t in range(n0 + 3):
                    if t < n0:
                        dve.wait_ge(scores_done, b * len(SCORES) + t + 1)
                        dve.wait_ge(exp_done, before(b, NT, t, DEEP))
                        link(nc.vector.memset(waited[:, t % 8:t % 8 + 1], 0.0))
                        mask(t, scores[t % 2][:], bias0[:, TILES0[t][2], :])
                    if t >= 3 and (t - 3) % 2 == 1:
                        evacuate(t - 3, (t - 3) // 16)
                for g in range(G0):
                    w, read = take(f"ctx{g}")
                    w4 = w.rearrange("p (c h k) -> p c h k", c=C, h=4)
                    link(nc.vector.reciprocal(rden0[:, g, :, :], w4[:, :, :, DH]))
                    linked()
                    nc.vector.tensor_tensor(ctxn[:, :, 4 * g:4 * g + 4, :], w4[:, :, :, 0:DH],
                                            rden0[:, g, :, :].unsqueeze(3).broadcast_to([P, C, 4, DH]), ALU.mult)\
                        .then_inc(read, 1)
                dve.wait_ge(x_loaded, b * 16 + 16)
                link(nc.vector.tensor_tensor(t_s[:], x_s[:], each_chunk(bo_s), ALU.add))
                linked()
                w, read = take("wo")
                nc.vector.tensor_tensor(flat(u_s), w[:], flat(t_s), ALU.add).then_inc(read, 1)
                dve.wait_ge(*out_of(b, "wo"))
                layernorm(0, u_s, x1, ln1g_s, ln1b_s)
                dve.wait_ge(ln_out, b * LN + 1)
                link(nc.vector.tensor_tensor(t_s[:], x1[:], each_chunk(b2_s), ALU.add))
                v_out(*take("v"))
                dve.wait_ge(adj_loaded, b * 32 + 64)
                link(nc.vector.tensor_tensor(adjmax, adj_s[:], adjT_s[:], ALU.max))
                linked()
                link(nc.vector.scalar_tensor_tensor(bias0[:], adjmax, 0.0, offdiag[:], ALU.is_le, ALU.mult))
                linked()
                w, read = take("down")
                nc.vector.tensor_tensor(flat(u_s), w[:], flat(t_s), ALU.add).then_inc(read, 1)
                dve.wait_ge(*out_of(b, "down"))
                layernorm(1, u_s, x2, ln2g_s, ln2b_s)
                dve.wait_ge(ln_out, b * LN + 2)
                nc.vector.tensor_tensor(flat(t_s), flat(x_s), flat(x2), ALU.add).then_inc(x_used, 1)
                dve.wait_ge(x_used, START + b + 1)
                layernorm(2, t_s, y0)
                for c in range(C + 1):
                    if c < C:
                        w, read = take(f"yw{c}")
                        dve.wait_ge(yhi, b * C + c + 1)
                        dve.wait_ge(ylo, before(b, C, c, 2))
                        nc.vector.tensor_tensor(yrest[:, c % 2, :], w[:], ysplit[:, c, 0, :], ALU.subtract)\
                            .then_inc(read, 1)
                    if c >= 1:
                        dve.wait_ge(*out_of(b, f"yw{c - 1}"))
                        dve.wait_ge(ymid, b * C + c)
                        nc.vector.tensor_tensor(ysplit[:, c - 1, 2, :], yrest[:, (c - 1) % 2, :],
                                                ysplit[:, c - 1, 1, :], ALU.subtract).then_inc(ylo, 1)
                w, read = take("relT")
                dve.wait_ge(ln_out, b * LN + 3)
                nc.vector.tensor_tensor(flat(t_s), w[:], flat(y0), ALU.add).then_inc(read, 1)
                dve.wait_ge(*out_of(b, "relT"))
                layernorm(3, t_s, y1)

                def attend(first, tiles, k0, buf):
                    made = []
                    for t in range(len(tiles) + 3):
                        if t < len(tiles):
                            _l, h, c = tiles[t]
                            n = SCORES.index(tiles[t][:2]) - n0
                            dve.wait_ge(d_copied, START + b * (1 + H3) + n + 1)
                            dve.wait_ge(masked_done, START + b * NT + first + max(t - 1, 0))
                            link(nc.vector.tensor_scalar(leaky[:, t % 2, :], targets[:, n % 2, :],
                                                         s_c[:, c, k0 + h:k0 + h + 1], 0.0, ALU.add, ALU.max))
                            made.append(chain[0])
                        if 1 <= t <= len(tiles):
                            dve.wait_ge(exp_done, before(b, NT, first + t - 1, DEEP))
                            dve.wait_ge(line_done, b * len(TILES2 + TILES3) + first - n0 + t)
                            link(nc.vector.memset(waited[:, t % 8:t % 8 + 1], 0.0))
                            dve.wait_ge(dve_chain, made[t - 1])
                            mask(first + t - 1, leaky[:, (t - 1) % 2, :], line[:, (t - 1) % 2, :], 1 - ALPHA)
                        if t >= 3 and (t - 3) % 2 == 1:
                            evacuate(first + t - 3, buf)

                w, read = take("s2")
                nc.vector.tensor_copy(s_c[:, :, 0], w[:, 0:C]).then_inc(read, 1)
                dve.wait_ge(*out_of(b, "s2"))
                attend(n0, TILES2, 0, 0)
                dve.wait_ge(exp_done, START + b * NT + n0 + C)
                link(nc.vector.reciprocal(rden[:, 0:C], den[:, n0:n0 + C]))
                linked()
                w, read = take("pv2")
                dve.wait_ge(ln_out, b * LN + 4)
                for c in range(C):
                    ins = nc.vector.scalar_tensor_tensor(t_s[:, c, :], w[:, c * P:(c + 1) * P], rden[:, c:c + 1],
                                                         y1[:, c, :], ALU.mult, ALU.add)
                    if c < C - 1:
                        link(ins)
                ins.then_inc(read, 1)
                dve.wait_ge(*out_of(b, "pv2"))
                layernorm(4, t_s, y2)
                w, read = take("h3")
                nc.vector.tensor_tensor(h3[:], chunks(w), each_chunk(b3r_s), ALU.add).then_inc(read, 1)
                w, read = take("s3")
                nc.vector.tensor_tensor(s_c[:, :, 1:1 + H3], w[:, 0:C * H3].rearrange("p (c h) -> p c h", h=H3),
                                        c3s[:].unsqueeze(1).broadcast_to([P, C, H3]), ALU.add).then_inc(read, 1)
                dve.wait_ge(*out_of(b, "s3"))
                attend(n0 + C, TILES3, 1, 1)
                dve.wait_ge(exp_done, START + b * NT + NT)
                link(nc.vector.reciprocal(rden[:, C:C + C * H3], den[:, n0 + C:NT]))
                linked()
                w, read = take("pv3")
                nc.vector.tensor_tensor(u_s.rearrange("p c (h k) -> p c h k", h=H3),
                                        w.rearrange("p (c h k) -> p c h k", c=C, h=H3),
                                        rden[:, C:C + C * H3].rearrange("p (h c) -> p c h", h=H3)
                                        .unsqueeze(3).broadcast_to([P, C, H3, DC]), ALU.mult).then_inc(read, 1)
                dve.wait_ge(*out_of(b, "pv3"))
                dve.wait_ge(ln_out, b * LN + 5)
                link(nc.vector.tensor_tensor(flat(t_s), flat(u_s), flat(y2), ALU.add))
                dve.wait_ge(y3_free, START + b)
                layernorm(5, t_s, y3)
                dve.wait_ge(ln_out, b * LN + LN)
                linked()


def kernel(**inputs):
    import concourse.bacc as bacc
    from concourse.bass_utils import run_bass_kernel_spmd

    v = {k: np.asarray(a) for k, a in inputs.items()}
    wqkv, bqkv = v["L0_gnn_Wqkv"], v["L0_gnn_bqkv"]

    def rows(a):
        return np.broadcast_to(a, (P, a.size))

    a3 = v["L3_gnn_a"]
    a3_blocks = np.zeros((P, 2 * H3), a3.dtype)
    for h in range(H3):
        a3_blocks[h * DC:(h + 1) * DC, h] = a3[h, :DC]
        a3_blocks[h * DC:(h + 1) * DC, H3 + h] = a3[h, DC:]
    arrays = {
        "x": v["x"], "xT": v["x"].transpose(0, 2, 1), "adj": v["adj"], "adjT": v["adj"].transpose(0, 2, 1),
        "wqT": wqkv[:D].T, "wkT": wqkv[D:2 * D].T,
        "wvT": wqkv[2 * D:].T, "bq": bqkv[:D, None],
        "bk": bqkv[D:2 * D, None], "bv": rows(bqkv[2 * D:]),
        "woT": v["L0_gnn_Wo"].T, "bo": rows(v["L0_gnn_bo"]), "w1T": v["L0_gnn_W1"].T,
        "b1": v["L0_gnn_b1"].reshape(F, P).T, "w2T": v["L0_gnn_W2"].T.reshape(F, P, D).transpose(1, 0, 2),
        "b2": rows(v["L0_gnn_b2"]), "ln1g": rows(v["L0_gnn_ln1_g"]), "ln1b": rows(v["L0_gnn_ln1_b"]),
        "ln2g": rows(v["L0_gnn_ln2_g"]), "ln2b": rows(v["L0_gnn_ln2_b"]),
        "rel_w": v["L1_gnn_weight"].transpose(1, 0, 2).reshape(D, R * D), "rel_b": v["L1_gnn_bias"][:, None],
        "w2g": v["L2_gnn_W"], "w2gT": v["L2_gnn_W"].T, "a2g": v["L2_gnn_a"].reshape(2, D).T,
        "w3T": v["L3_gnn_W"].T, "w3": v["L3_gnn_W"], "b3c": v["L3_gnn_b"][:, None], "b3r": rows(v["L3_gnn_b"]),
        "a3": a3_blocks,
    }
    nc = bacc.Bacc("TRN2", target_bir_lowering=False, num_devices=1)
    data, args = {}, []
    for name, a in arrays.items():
        data[f"{name}_in"] = np.ascontiguousarray(a)
        args.append(nc.dram_tensor(f"{name}_in", a.shape, mybir.dt.from_np(a.dtype), kind="ExternalInput").ap())
    args.append(nc.dram_tensor("parts", (P, 3, 2, N), mybir.dt.bfloat16, kind="Internal").ap())
    args.append(nc.dram_tensor("out", v["x"].shape, mybir.dt.float32, kind="ExternalOutput").ap())
    build(nc, *args)
    return run_bass_kernel_spmd(nc, [data], core_ids=[0]).results[0]["out"]
```
